# Optimizing a Trainium2 kernel written in Bass

```python
import numpy as np
import jax
import jax.numpy as jnp

def _softmax(x, axis=-1):
    return jax.nn.softmax(x, axis=axis)

def _gelu(x):
    return jax.nn.gelu(x, approximate=True)

def _silu(x):
    return jax.nn.silu(x)

def _sigmoid(x):
    return jax.nn.sigmoid(x)

def _layernorm(x, axis=-1, eps=1e-05):
    m = jnp.mean(x, axis=axis, keepdims=True)
    v = jnp.var(x, axis=axis, keepdims=True)
    return (x - m) / jnp.sqrt(v + eps)

def _scatter_add(tgt, idx, src, axis=0):
    return tgt.at[idx].add(src)

def _segment_sum(src, seg, n):
    return jax.ops.segment_sum(src, seg, n)
kernel_name = 'mk_vit_tower_postln_d1_tok_img1024_r4_876ffc'

def setup_inputs(seed: int=0):
    np.random.seed(seed)
    _w = jnp.asarray

    def _rec_inputs():
        import jax
        import jax.numpy as jnp
        _rk = jax.random.key(seed)
        x = -0.000356955 + 1 * jax.random.normal(jax.random.fold_in(_rk, 1), (128, 3, 64, 64), jnp.float32)
        return x
    x = _rec_inputs()

    def _L0_tok_setup():
        import jax, jax.numpy as jnp
        import numpy as np
        PATCH = 16
        EMBED = 256
        key = jax.random.key(seed)
        kx, kw = jax.random.split(key, 2)
        x = jax.random.normal(kx, (128, 3, 224, 224), dtype=jnp.float32)
        in_feat = PATCH * PATCH * 3
        W = jax.random.normal(kw, (EMBED, in_feat), dtype=jnp.float32) * 0.02
        b = jnp.zeros((EMBED,), dtype=jnp.float32)
        return {'x': x, 'W': W, 'b': b}
    _L0_tok_all = _L0_tok_setup()
    _L0_tok_in = {k: v for k, v in _L0_tok_all.items() if k in ('W', 'b')}
    del _L0_tok_all

    def _L0_attn_setup():
        import jax, jax.numpy as jnp
        import numpy as np
        DIM = 256
        HEADS = 16
        HEAD_DIM = DIM // HEADS
        NUM_FILTERS = 4
        NUM_TAPS = 101
        RES = 128

        def _fir_fft(c, sig):
            R = sig.shape[0]
            L = R + c.shape[0] - 1
            out = jnp.fft.ifft(jnp.fft.fft(sig, n=L) * jnp.fft.fft(c, n=L)).real
            return out[:R]
        key = jax.random.key(seed)
        ks = jax.random.split(key, 5)
        B, S = (2, 512)
        x = jax.random.normal(ks[0], (B, S, DIM), dtype=jnp.float32)
        Wqkv = jax.random.normal(ks[1], (3 * DIM, DIM), dtype=jnp.float32) * DIM ** (-0.5)
        Wout = jax.random.normal(ks[2], (DIM, DIM), dtype=jnp.float32) * DIM ** (-0.5)
        Wpos = jax.random.normal(ks[3], (HEADS, NUM_FILTERS), dtype=jnp.float32) * 0.5
        coeffs = jax.random.normal(ks[4], (NUM_FILTERS, NUM_TAPS), dtype=jnp.float32) * 0.05
        return {'x': x, 'Wqkv': Wqkv, 'Wout': Wout, 'Wpos': Wpos, 'coeffs': coeffs}
    _L0_attn_all = _L0_attn_setup()
    _L0_attn_in = {k: v for k, v in _L0_attn_all.items() if k in ('Wqkv', 'Wout', 'Wpos', 'coeffs')}
    del _L0_attn_all

    def _L0_ffn_setup():
        import jax, jax.numpy as jnp
        import numpy as np
        from jax import lax
        T, B, I, M, O = (64, 64, 256, 256, 256)

        def _xavier(key, shape):
            fan_out, fan_in = shape
            limit = float(np.sqrt(6.0 / (fan_in + fan_out)))
            return jax.random.uniform(key, shape, jnp.float32, -limit, limit)
        key = jax.random.key(seed)
        ks = jax.random.split(key, 9)
        x = jax.random.normal(ks[0], (T, B, I), jnp.float32)
        return {'x': x, 'wf': _xavier(ks[1], (M, I)), 'uf': _xavier(ks[2], (M, M)), 'bf': jnp.zeros((M,), jnp.float32), 'wi': _xavier(ks[3], (M, I)), 'ui': _xavier(ks[4], (M, M)), 'bi': jnp.zeros((M,), jnp.float32), 'wc': _xavier(ks[5], (M, I)), 'uc': _xavier(ks[6], (M, M)), 'bc': jnp.zeros((M,), jnp.float32), 'wo': _xavier(ks[7], (O, I)), 'uo': _xavier(ks[8], (O, M)), 'bo': jnp.zeros((O,), jnp.float32), 'in_c': jnp.zeros((M,), jnp.float32)}
    _L0_ffn_all = _L0_ffn_setup()
    _L0_ffn_in = {k: v for k, v in _L0_ffn_all.items() if k in ('wf', 'uf', 'bf', 'wi', 'ui', 'bi', 'wc', 'uc', 'bc', 'wo', 'uo', 'bo', 'in_c')}
    del _L0_ffn_all
    return {'x': x, 'L0_tok_W': _L0_tok_in['W'], 'L0_tok_b': _L0_tok_in['b'], 'L0_attn_Wqkv': _L0_attn_in['Wqkv'], 'L0_attn_Wout': _L0_attn_in['Wout'], 'L0_attn_Wpos': _L0_attn_in['Wpos'], 'L0_attn_coeffs': _L0_attn_in['coeffs'], 'L0_ffn_wf': _L0_ffn_in['wf'], 'L0_ffn_uf': _L0_ffn_in['uf'], 'L0_ffn_bf': _L0_ffn_in['bf'], 'L0_ffn_wi': _L0_ffn_in['wi'], 'L0_ffn_ui': _L0_ffn_in['ui'], 'L0_ffn_bi': _L0_ffn_in['bi'], 'L0_ffn_wc': _L0_ffn_in['wc'], 'L0_ffn_uc': _L0_ffn_in['uc'], 'L0_ffn_bc': _L0_ffn_in['bc'], 'L0_ffn_wo': _L0_ffn_in['wo'], 'L0_ffn_uo': _L0_ffn_in['uo'], 'L0_ffn_bo': _L0_ffn_in['bo'], 'L0_ffn_in_c': _L0_ffn_in['in_c']}

def reference(x, L0_tok_W, L0_tok_b, L0_attn_Wqkv, L0_attn_Wout, L0_attn_Wpos, L0_attn_coeffs, L0_ffn_wf, L0_ffn_uf, L0_ffn_bf, L0_ffn_wi, L0_ffn_ui, L0_ffn_bi, L0_ffn_wc, L0_ffn_uc, L0_ffn_bc, L0_ffn_wo, L0_ffn_uo, L0_ffn_bo, L0_ffn_in_c):
    import jax
    import jax.numpy as jnp

    def _L0_tok_ref(x, W, b):
        import jax, jax.numpy as jnp
        import numpy as np
        PATCH = 16
        EMBED = 256
        p = PATCH
        B, C, H, Wd = x.shape
        gh, gw = (H // p, Wd // p)
        patches = x.reshape(B, C, gh, p, gw, p).transpose(0, 1, 2, 4, 3, 5)
        patches = patches.reshape(B, gh * gw, p * p * C)
        return jnp.einsum('bnk,ek->bne', patches, W) + b

    def _L0_attn_ref(x, Wqkv, Wout, Wpos, coeffs):
        import jax, jax.numpy as jnp
        import numpy as np
        DIM = 256
        HEADS = 16
        HEAD_DIM = DIM // HEADS
        NUM_FILTERS = 4
        NUM_TAPS = 101
        RES = 128

        def _fir_fft(c, sig):
            R = sig.shape[0]
            L = R + c.shape[0] - 1
            out = jnp.fft.ifft(jnp.fft.fft(sig, n=L) * jnp.fft.fft(c, n=L)).real
            return out[:R]
        B, S, D = x.shape
        scale = HEAD_DIM ** (-0.5)
        proto = jnp.linspace(0.0, 1.0, RES).astype(x.dtype)
        table = jax.vmap(_fir_fft, in_axes=(0, None))(coeffs, proto).T
        r = jnp.arange(S)
        rel = jnp.abs(r[None, :] - r[:, None]).astype(jnp.float32) / max(S - 1, 1)
        idx = jnp.clip(jnp.round(rel * (RES - 1)).astype(jnp.int32), 0, RES - 1)
        pos_feat = table[idx]
        pos_bias = jnp.einsum('ijf,hf->hij', pos_feat, Wpos)
        qkv = jnp.einsum('bsd,ed->bse', x, Wqkv)
        q, k, v = jnp.split(qkv, 3, axis=-1)
        q = q.reshape(B, S, HEADS, HEAD_DIM)
        k = k.reshape(B, S, HEADS, HEAD_DIM)
        v = v.reshape(B, S, HEADS, HEAD_DIM)
        logits = jnp.einsum('bihd,bjhd->bhij', q, k) * scale + pos_bias[None]
        attn = jax.nn.softmax(logits, axis=-1)
        out = jnp.einsum('bhij,bjhd->bihd', attn, v).reshape(B, S, D)
        return jnp.einsum('bsd,ed->bse', out, Wout)

    def _L0_ffn_ref(x, wf, uf, bf, wi, ui, bi, wc, uc, bc, wo, uo, bo, in_c):
        import jax, jax.numpy as jnp
        import numpy as np
        from jax import lax
        T, B, I, M, O = (64, 64, 256, 256, 256)

        def _xavier(key, shape):
            fan_out, fan_in = shape
            limit = float(np.sqrt(6.0 / (fan_in + fan_out)))
            return jax.random.uniform(key, shape, jnp.float32, -limit, limit)
        batch = x.shape[1]
        c0 = jnp.broadcast_to(in_c, (batch, in_c.shape[0]))

        def step(c, xt):
            ft = jax.nn.sigmoid(xt @ wf.T + c @ uf.T + bf)
            it = jax.nn.sigmoid(xt @ wi.T + c @ ui.T + bi)
            gt = jnp.tanh(xt @ wc.T + c @ uc.T + bc)
            c = ft * c + it * gt
            return (c, None)
        c_final, _ = lax.scan(step, c0, x)
        h = jnp.tanh(jnp.einsum('tbi,oi->tbo', x, wo) + c_final @ uo.T + bo)
        return h
    h = _L0_tok_ref(x, L0_tok_W, L0_tok_b)
    h = _layernorm(h + _L0_attn_ref(h, L0_attn_Wqkv, L0_attn_Wout, L0_attn_Wpos, L0_attn_coeffs), axis=-1)
    h = _layernorm(h + _L0_ffn_ref(h, L0_ffn_wf, L0_ffn_uf, L0_ffn_bf, L0_ffn_wi, L0_ffn_ui, L0_ffn_bi, L0_ffn_wc, L0_ffn_uc, L0_ffn_bc, L0_ffn_wo, L0_ffn_uo, L0_ffn_bo, L0_ffn_in_c), axis=-1)
    return h

_drawn_inputs = setup_inputs


def setup_inputs(seed=0):
    import zlib

    import numpy as np

    out = dict(_drawn_inputs(seed))
    spreads = {'L0_tok_b': (0.0, 0.1),
     'L0_ffn_bf': (0.0, 0.678),
     'L0_ffn_bi': (0.0, 0.632),
     'L0_ffn_bc': (0.0, 0.1),
     'L0_ffn_bo': (0.0, 0.1),
     'L0_ffn_in_c': (0.0, 0.8)}
    factors = {'L0_attn_Wpos': 3.375, 'L0_attn_coeffs': 4.893}
    for name, (base, spread) in spreads.items():
        noise = np.random.default_rng([zlib.crc32(name.encode()), seed]).standard_normal(out[name].shape)
        drawn = base * np.exp(spread * noise) if base else spread * noise
        out[name] = jnp.asarray(drawn.astype(out[name].dtype))
    for name, factor in factors.items():
        out[name] = (out[name] * factor).astype(out[name].dtype)
    return out
```

```python
from contextlib import ExitStack

import concourse.bass as bass
from concourse import mybir
from concourse.alu_op_type import AluOpType as ALU

ACT = mybir.ActivationFunctionType
F32 = mybir.dt.float32
F16 = mybir.dt.float16
AX_X = mybir.AxisListType.X

P = 128
D = 256
KC = D // P
S = 16
B = 8
TOK = B * S
G = 16
H = 16
HD = D // H
HC = H // KC
PC = 6
NG = 3
TAPS, RES, NF = 101, 128, 4
VW = HD + 1

WSCALE = 256.0
UNSCALE = 1.0 / WSCALE
EPS = 1e-5

K_XHI_A, K_XHI_B = -3, -2
EMB = {-1: (0, 1), 0: (1, 3), 1: (3, 5), 4: (5, 6)}
K_H0 = 5
K_TH0 = 8
K_H0T = 9
K_Q, K_K = 10, 11
K_QK = 12
K_QX = (12, 13)
QX_RUNS = ((0, 2), (2, 8))
K_V = 13
K_VOUT = 14
K_S0, K_S1 = 14, 15
K_SM = 16
K_EXP = 17
K_TP = 18
K_PT = 19
K_PX = (19, 20)
PX_RUNS = ((0, 4), (4, 8))
K_PV0, K_PV1 = 21, 22
K_O = 23
K_OHL = 24
K_TO = 25
K_OT = 26
K_WO = 27
K_LN = 29
K_H1 = 30
K_H1HL = 31
K_TH1 = 32
K_H1T = 33
XP = {34: (0, 2), 35: (2, 3), 36: (3, 6)}
K_SCAN = 37
SLOTS = 2 * B
PAIRS = G // 2


def at_least(eng, sem, value):
    if isinstance(value, int) and value <= 0:
        return
    eng.wait_ge(sem, value)


def upto(value):
    return min(value, G) if isinstance(value, int) else value


def run_slots(eng, slot):
    first = -((K_SCAN - K_XHI_A + SLOTS - 1) // SLOTS)
    full = PAIRS - (K_SCAN + SLOTS - 1 - K_XHI_A) // SLOTS
    for j in range(first, 0):
        for q in range(SLOTS):
            slot(j, q)
    with eng.Fori(0, full) as j:
        for q in range(SLOTS):
            slot(j, q)
    for j in range(full, PAIRS):
        for q in range(SLOTS):
            slot(j, q)


def group_of(j, q, k):
    d, r = divmod(K_SCAN + q - k, B)
    if r:
        return None
    if isinstance(j, int):
        g = 2 * j + d
        return (g, d % 2) if 0 <= g < G else None
    return (j * 2 + d, d % 2)


def vit_layer(nc, xT, w_tok, w_qkv, w_out, w_gx, w_gu, w_ox, w_ou, brow, in_c, coeffs, wpos,
              protoT, pick, blocks, eye, out):
    with ExitStack() as ctx:
        def sb(name, shape, dt):
            return ctx.enter_context(nc.sbuf_tensor(name, shape, dt))

        def bank(name):
            return ctx.enter_context(nc.psum_tensor(name, [P, 512], F32))

        def sem(name):
            return ctx.enter_context(nc.semaphore(name))

        w_shapes = {"tok": PC * D, "qkv": KC * 3 * D, "out": KC * D, "gx": KC * NG * D,
                    "gu": KC * NG * D, "ox": KC * D, "ou": KC * D}
        w_dram = {"tok": w_tok, "qkv": w_qkv, "out": w_out, "gx": w_gx, "gu": w_gu, "ox": w_ox, "ou": w_ou}
        w32 = {n: sb("w32_" + n, [P, c], F32) for n, c in w_shapes.items()}
        whl = {n: sb("whl_" + n, [P, 2, c], F16) for n, c in w_shapes.items()}
        NB = D + NG * D + D
        brow32 = sb("brow32", [1, NB], F32)
        brow_lo = sb("brow_lo", [1, NB], F16)
        bias2 = sb("bias2", [2, NB], F16)
        ones2 = sb("ones2", [2, P], F16)

        eye32 = sb("eye32", [P, P], F32)
        eye16 = sb("eye16", [P, P], F16)
        eyew = sb("eyew", [P, P], F16)
        coef_sb = sb("coef_sb", [NF, TAPS], F32)
        wpos_sb = sb("wpos_sb", [NF, H], F32)
        proto_sb = sb("proto_sb", [TAPS, S], F32)
        pick_sb = sb("pick_sb", [P, S, S], F32)
        m1 = sb("m1", [TAPS, H, S], F32)
        ed = sb("ed", [P, KC, S], F32)
        picked = sb("picked", [P, S, S], F32)
        posb = sb("posb", [P, KC, S], F32)
        block_sb = sb("block_sb", [P, HC], F32)
        minus_half = sb("minus_half", [P, 1], F32)
        eps = sb("eps", [P, 1], F32)

        x32 = sb("x32", [P, 2, PC, TOK], F32)
        xhl = sb("xhl", [P, 2, PC, TOK], F16)
        hall = sb("hall", [P, G * D], F32)
        h0hl = sb("h0hl", [P, 2, D], F16)
        h0T = sb("h0T", [P, 2, KC, TOK], F16)
        qT = sb("qT", [P, 2, KC, S, B], F16)
        kT = sb("kT", [P, 2, KC, TOK], F16)
        v = sb("v", [P, 2, 2, H, VW], F16)
        qx = sb("qx", [P, 2, KC, HC * S * B], F16)
        sc = sb("sc", [P, KC, B, S], F32)
        mx = sb("mx", [P, KC, B], F32)
        scm = sb("scm", [P, KC, B, S], F32)
        e32 = sb("e32", [P, KC * TOK], F32)
        ehl = sb("ehl", [P, 2, KC * TOK], F16)
        pT = sb("pT", [P, 2, KC, S, HC], F16)
        px = sb("px", [P, 2, KC, B * S * HC], F16)
        rs = sb("rs", [P, H], F32)
        o32 = sb("o32", [P, D], F32)
        ohl = sb("ohl", [P, 2, D], F16)
        oT = sb("oT", [P, 2, KC, TOK], F16)
        r1 = sb("r1", [P, D], F32)
        stats = sb("stats", [P, 6], F32)
        mv = sb("mv", [P, 2], F32)
        veps = sb("veps", [P, 1], F32)
        rstd = sb("rstd", [P, 1], F32)
        h1hl = sb("h1hl", [P, 2, D], F16)
        h1T = sb("h1T", [P, 2 * KC * TOK], F16)
        h1Tall = sb("h1Tall", [P, G * 2 * KC * TOK], F16)

        inc_sb = sb("inc_sb", [P, KC], F32)
        s32 = sb("s32", [P, KC, S], F32)
        shi = sb("shi", [P, KC, S], F16)
        slo = sb("slo", [P, KC, S], F16)
        gate = sb("gate", [P, KC, NG * S], F32)
        keepf = sb("keepf", [P, KC, S], F32)
        inp = sb("inp", [P, KC, S], F32)

        cx = sb("cx", [P, 2, KC, B, S], F16)
        y32 = sb("y32", [P, D], F32)
        yhl = sb("yhl", [P, 2, D], F16)
        t32 = sb("t32", [P, 4, D], F32)
        r2 = sb("r2", [P, 4, D], F32)
        res = sb("res", [P, 4, D], F32)
        stats2 = sb("stats2", [P, 4, 6], F32)
        mv2 = sb("mv2", [P, 4, 2], F32)
        veps2 = sb("veps2", [P, 4], F32)
        rstd2 = sb("rstd2", [P, 4], F32)

        gsum = [[bank(f"gsum{p}{c}") for c in range(KC)] for p in range(2)]
        bankA, bankB, bankC, bankD = bank("bankA"), bank("bankB"), bank("bankC"), bank("bankD")
        tail_banks = gsum[0] + gsum[1]
        emb_ps = bankA[:, 0:D]
        s_ps = bankB[:, 0:KC * TOK]
        to_ps = bankB[:].bitcast(F16)[:, 0:512].rearrange("p (a c t) -> p a c t", a=2, c=KC)
        wo_ps = bankB[:, 0:D]
        th_ps = bankC[:].bitcast(F16).rearrange("p (w a c t) -> p w a c t", w=2, a=2, c=KC)
        v_ps = bankC[:, 0:D]
        q_ps, k_ps = bankD[:, 0:KC * TOK], bankD[:, KC * TOK:]
        pv_ps = bankD[:, 0:H * VW].rearrange("p (h w) -> p h w", w=VW)

        w_in = {n: sem("w_in_" + n) for n in w_shapes}
        small_in = sem("small_in")
        w_hi = {n: sem("w_hi_" + n) for n in w_shapes}
        w_lo = {n: sem("w_lo_" + n) for n in w_shapes}
        const_set, eye_set = sem("const_set"), sem("eye_set")
        b_hi, b_lo, b_row = sem("b_hi"), sem("b_lo"), sem("b_row")
        pos_m1, pos_m1x, pos_e, pos_ex, pos_pick, pos_set = (
            sem("pos_m1"), sem("pos_m1x"), sem("pos_e"), sem("pos_ex"), sem("pos_pick"), sem("pos_set"))
        x_in = [sem("x_in0"), sem("x_in1")]
        x_hi, x_split = sem("x_hi"), sem("x_split")
        emb_done, h0_ready, h0_split = sem("emb_done"), sem("h0_ready"), sem("h0_split")
        th0_done, h0T_ready = sem("th0_done"), sem("h0T_ready")
        qk_done, qk_hi, qk_lo, qx_ready = sem("qk_done"), sem("qk_hi"), sem("qk_lo"), sem("qx_ready")
        v_done, v_hi, v_ready = sem("v_done"), sem("v_hi"), sem("v_ready")
        s_done, sc_ready, mx_ready, scm_ready = sem("s_done"), sem("sc_ready"), sem("mx_ready"), sem("scm_ready")
        e_ready, e_hi, e_split = sem("e_ready"), sem("e_hi"), sem("e_split")
        tp_done, pT_ready, px_ready = sem("tp_done"), sem("pT_ready"), sem("px_ready")
        pv_done, rs_ready, o_ready, o_hi, o_split = (
            sem("pv_done"), sem("rs_ready"), sem("o_ready"), sem("o_hi"), sem("o_split"))
        to_done, oT_ready = sem("to_done"), sem("oT_ready")
        wo_done, r1_ready, st1_ready, st1_seen, mv1_ready, ve1_ready, rstd1_ready = (
            sem("wo_done"), sem("r1_ready"), sem("st1_ready"), sem("st1_seen"), sem("mv1_ready"), sem("ve1_ready"),
            sem("rstd1_ready"))
        h1_ready, h1_hi, h1_split = sem("h1_ready"), sem("h1_hi"), sem("h1_split")
        th1_done, h1T_ready, h1T_kept, xp_done = (
            sem("th1_done"), sem("h1T_ready"), sem("h1T_kept"), sem("xp_done"))
        pre = [sem(f"pre{c}") for c in range(KC)]
        gates = [sem(f"gates{c}") for c in range(KC)]
        addends = [sem(f"addends{c}") for c in range(KC)]
        s_hi = [sem(f"s_hi{c}") for c in range(KC)]
        s_32 = [sem(f"s_32{c}") for c in range(KC)]
        s_lo = [sem(f"s_lo{c}") for c in range(KC)]
        cx_ready, y_done, y_ready, y_hi, y_split = (
            sem("cx_ready"), sem("y_done"), sem("y_ready"), sem("y_hi"), sem("y_split"))
        o2_done, t_ready, r2_ready, st2_ready, mv2_ready, ve2_ready, rstd2_ready, res_ready = (
            sem("o2_done"), sem("t_ready"), sem("r2_ready"), sem("st2_ready"), sem("mv2_ready"),
            sem("ve2_ready"), sem("rstd2_ready"), sem("res_ready"))
        out_in = [sem(f"out_in{i}") for i in range(4)]

        block = ctx.enter_context(nc.Block())

        def scaled(n):
            if n == "qkv":
                w = lambda t: t.rearrange("p (k e) -> p k e", k=KC)
                return [(lambda t: w(t)[:, :, 0:D], WSCALE * HD ** -0.5), (lambda t: w(t)[:, :, D:3 * D], WSCALE)]
            if n in ("gx", "gu"):
                f = 1.0 if n == "gx" else 0.5
                w = lambda t: t.rearrange("p (k e) -> p k e", e=NG * P)
                return [(lambda t: w(t)[:, :, 0:2 * P], WSCALE * 0.5 * f), (lambda t: w(t)[:, :, 2 * P:], WSCALE * f)]
            return [(lambda t: t, WSCALE * (0.5 if n == "ou" else 1.0))]

        bias_parts = [(0, D, WSCALE)]
        for c in range(KC):
            o = D + c * NG * P
            bias_parts += [(o, o + 2 * P, WSCALE * 0.5), (o + 2 * P, o + 3 * P, WSCALE)]
        bias_parts += [(D + NG * D, NB, WSCALE)]

        @block.sync
        def _(sp):
            xg = xT.rearrange("p (g c) -> p g c", g=G)
            sp.dma_start(x32[:, 0].rearrange("p c t -> p (c t)"), xg[:, 0, :]).then_inc(x_in[0], 16)
            sp.dma_start(w32["tok"][:], w_tok).then_inc(w_in["tok"], 16)
            for t, a in ((brow32, brow), (eye32, eye), (coef_sb, coeffs), (wpos_sb, wpos), (proto_sb, protoT),
                         (inc_sb, in_c), (block_sb, blocks)):
                sp.dma_start(t[:], a).then_inc(small_in, 16)
            sp.dma_start(pick_sb[:].rearrange("p j d -> p (j d)"), pick).then_inc(small_in, 16)
            for n in ("qkv", "out", "gx", "gu", "ox", "ou"):
                sp.dma_start(w32[n][:], w_dram[n]).then_inc(w_in[n], 16)
            sp.wait_ge(b_lo, len(bias_parts))
            sp.dma_start(bias2[1:2, :], brow_lo[:]).then_inc(b_row, 16)

            def load_x(j, g, p):
                at_least(sp, x_split, g * 2 - 2)
                sp.dma_start(x32[:, p].rearrange("p c t -> p (c t)"),
                             xT[:, bass.ds(g * (PC * TOK), PC * TOK)]).then_inc(x_in[p], 16)

            def keep_h1T(j, g, p):
                sp.wait_ge(h1T_ready, g + 1)
                w = 2 * KC * TOK
                sp.dma_start(h1Tall[:, bass.ds(g * w, w)], h1T[:]).then_inc(h1T_kept, 16)

            def slot(j, q):
                for k, stage in ((K_H1T, keep_h1T), (-B, load_x)):
                    at = group_of(j, q, k)
                    if at is None or (stage is load_x and isinstance(at[0], int) and at[0] == 0):
                        continue
                    stage(j, *at)

            run_slots(sp, slot)

            for g in range(G):
                sp.wait_ge(res_ready, g + 1)
                sp.dma_start(out[g * TOK:(g + 1) * TOK, :], res[:, g % 4]).then_inc(out_in[g % 4], 16)
            for i in range(4):
                sp.wait_ge(out_in[i], 16 * (G // 4))

        @block.scalar
        def _(act):
            def weight_hi(n):
                act.wait_ge(w_in[n], 16)
                for part, scale in scaled(n):
                    nc.scalar.activation(part(whl[n][:, 0]), part(w32[n][:]), ACT.Copy, scale=scale).then_inc(w_hi[n], 1)

            def prepare(T):
                if T == K_XHI_A:
                    act.wait_ge(small_in, 16 * 8)
                    for lo, hi, scale in bias_parts:
                        nc.scalar.activation(bias2[0:1, lo:hi], brow32[:, lo:hi], ACT.Copy, scale=scale).then_inc(b_hi, 1)
                    nc.scalar.activation(eye16[:], eye32[:], ACT.Copy).then_inc(eye_set, 1)
                    nc.scalar.activation(eyew[:], eye32[:], ACT.Copy, scale=WSCALE).then_inc(eye_set, 1)
                for k, n in ((K_XHI_A, "tok"), (3, "qkv"), (K_VOUT, "out"), (20, "gx"), (22, "gu"), (24, "ox"), (25, "ou")):
                    if T == k:
                        weight_hi(n)

            def x_pair_hi(half):
                def stage(j, g, p):
                    if half == 0:
                        act.wait_ge(x_in[p], g * 8 + (16 - 8 * p))
                    at_least(act, emb_done, g)
                    c = slice(half * PC // 2, (half + 1) * PC // 2)
                    nc.scalar.activation(xhl[:, 0, c], x32[:, p, c], ACT.Copy).then_inc(x_hi, 1)
                return stage

            def h0_out(j, g, p):
                act.wait_ge(emb_done, g + 1)
                at_least(act, th0_done, g)
                nc.scalar.activation(hall[:, bass.ds(g * D, D)], emb_ps, ACT.Copy, scale=UNSCALE)
                nc.scalar.activation(h0hl[:, 0], emb_ps, ACT.Copy, scale=UNSCALE).then_inc(h0_ready, 1)

            def h0T_out(j, g, p):
                act.wait_ge(th0_done, g + 1)
                at_least(act, th1_done, g - 2)
                at_least(act, v_done, g)
                nc.scalar.activation(h0T[:], th_ps[:, 0], ACT.Copy).then_inc(h0T_ready, 1)

            def qk_out(j, g, p):
                act.wait_ge(qk_done, g + 1)
                at_least(act, s_done, g)
                nc.scalar.activation(kT[:, 0], k_ps.rearrange("p (c t) -> p c t", c=KC), ACT.Copy, scale=UNSCALE)
                nc.scalar.activation(qT[:, 0].rearrange("p c s b -> p c b s"),
                                     q_ps.rearrange("p (c b s) -> p c b s", c=KC, b=B), ACT.Copy,
                                     scale=UNSCALE).then_inc(qk_hi, 1)

            def v_out(j, g, p):
                act.wait_ge(v_done, g + 1)
                at_least(act, pv_done, g - 1)
                nc.scalar.activation(v[:, p, 0, :, 0:HD], v_ps.rearrange("p (h w) -> p h w", w=HD), ACT.Copy,
                                     scale=UNSCALE).then_inc(v_hi, 1)

            def exponential(j, g, p):
                act.wait_ge(scm_ready, g + 1)
                at_least(act, e_split, g)
                nc.scalar.activation(e32[:], scm[:].rearrange("p c b j -> p (c b j)"), ACT.Exp).then_inc(e_ready, 1)
                act.wait_ge(e_ready, g + 1)
                at_least(act, tp_done, g)
                nc.scalar.activation(ehl[:, 0], e32[:], ACT.Copy).then_inc(e_hi, 1)

            def pT_out(j, g, p):
                act.wait_ge(tp_done, g + 1)
                at_least(act, pv_done, g)
                nc.scalar.activation(pT[:].rearrange("p a c s h -> p (a c) h s"),
                                     th_ps[:, 0].rearrange("p a c (h s) -> p (a c) h s", h=HC), ACT.Copy).then_inc(pT_ready, 1)

            def o_pair_hi(j, g, p):
                act.wait_ge(o_ready, g + 1)
                at_least(act, to_done, g)
                nc.scalar.activation(ohl[:, 0], o32[:], ACT.Copy).then_inc(o_hi, 1)

            def oT_out(j, g, p):
                act.wait_ge(to_done, g + 1)
                at_least(act, wo_done, g)
                nc.scalar.activation(oT[:], to_ps, ACT.Copy).then_inc(oT_ready, 1)

            def h1_pair_hi(j, g, p):
                act.wait_ge(h1_ready, g + 1)
                at_least(act, th1_done, g)
                nc.scalar.activation(h1hl[:, 0], hall[:, bass.ds(g * D, D)], ACT.Copy).then_inc(h1_hi, 1)

            def h1T_out(j, g, p):
                act.wait_ge(th1_done, g + 1)
                act.wait_ge(th0_done, upto(g + 4))
                at_least(act, xp_done, g)
                at_least(act, h1T_kept, g * 16)
                nc.scalar.activation(h1T[:], th_ps[:, 1].rearrange("p a c t -> p (a c t)"), ACT.Copy).then_inc(h1T_ready, 1)

            stages = ((K_H1T, h1T_out), (K_H1HL, h1_pair_hi), (K_OT, oT_out), (K_OHL, o_pair_hi), (K_PT, pT_out),
                      (K_EXP, exponential), (K_VOUT, v_out), (K_QK, qk_out), (K_H0T, h0T_out), (K_H0, h0_out),
                      (K_XHI_A, x_pair_hi(0)), (K_XHI_B, x_pair_hi(1)))

            def slot(j, q):
                if not isinstance(j, int) or j >= 0:
                    par, u = q // B, q % B
                    done = j * SLOTS + (q + 1)
                    for c in range(KC):
                        act.wait_ge(pre[c], done)
                        nc.scalar.activation(gate[:, c], gsum[par][c][:, u * NG * S:(u + 1) * NG * S], ACT.Tanh,
                                             scale=UNSCALE).then_inc(gates[c], 1)
                if isinstance(j, int):
                    prepare(SLOTS * j + K_SCAN + q)
                for k, stage in stages:
                    at = group_of(j, q, k)
                    if at is not None:
                        stage(j, *at)

            run_slots(act, slot)

            act.wait_ge(y_done, 1)
            nc.scalar.activation(y32[:], bankA[:, 0:D], ACT.Copy, scale=UNSCALE).then_inc(y_ready, 1)
            act.wait_ge(y_ready, 1)
            nc.scalar.activation(yhl[:, 0], y32[:], ACT.Copy).then_inc(y_hi, 1)
            for g in range(G):
                act.wait_ge(o2_done, g + 1)
                at_least(act, r2_ready, g - 3)
                nc.scalar.activation(t32[:, g % 4], tail_banks[g % 4][:, 0:D], ACT.Tanh, scale=UNSCALE).then_inc(t_ready, 1)

        @block.tensor
        def _(pe):
            PAIR = ((0, 0), (0, 1), (1, 0))

            def mm(o, lhsT, rhs, start):
                return nc.tensor.matmul(o, lhsT, rhs, start=start, stop=False, skip_group_check=True)

            wt = {n: whl[n][:].rearrange("p a (k e) -> p a k e", k=PC if n == "tok" else KC) for n in w_shapes}
            w_parts = {n: len(scaled(n)) for n in w_shapes}

            def weights(n):
                pe.wait_ge(w_lo[n], w_parts[n])

            def filling(T):
                if T == K_XHI_A:
                    pe.wait_ge(small_in, 16 * 8)
                    nc.tensor.matmul(bankB[0:TAPS, 0:H], coef_sb[:], wpos_sb[:], start=True, stop=True).then_inc(pos_m1, 1)
                    pe.wait_ge(pos_m1x, 1)
                    for c in range(KC):
                        last = nc.tensor.matmul(bankB[:, c * S:(c + 1) * S], m1[:, c * HC:(c + 1) * HC, :], proto_sb[:],
                                                start=True, stop=True)
                    last.then_inc(pos_e, 1)
                    pe.wait_ge(pos_ex, 1)
                    weights("tok")
                    pe.wait_ge(b_row, 16)
                    pe.wait_ge(b_hi, len(bias_parts))
                    pe.wait_ge(const_set, 1)
                    pe.wait_ge(eye_set, 2)
                for k, n in ((K_Q, "qkv"), (K_WO, "out"), (min(XP), "gx"), (K_SCAN - 1, "gu")):
                    if T == k:
                        weights(n)

            def embed(lo, hi):
                def stage(j, g, p):
                    if lo == 0:
                        at_least(pe, h0_ready, g)
                    pe.wait_ge(x_split, g * 2 + (1 if hi <= PC // 2 else 2))
                    for c in range(lo, hi):
                        for a, b in PAIR:
                            last = mm(emb_ps, xhl[:, a, c], wt["tok"][:, b, c], c == 0 and a == 0 and b == 0)
                    if hi == PC:
                        mm(emb_ps, ones2[:], bias2[:, 0:D], False).then_inc(emb_done, 1)
                return stage

            def transpose_h0(j, g, p):
                pe.wait_ge(h0_split, g + 1)
                at_least(pe, v_ready, g)
                for a in range(2):
                    for c in range(KC):
                        last = nc.tensor.transpose(th_ps[:, 0, a, c], h0hl[:, a, c * P:(c + 1) * P], eye16[:])
                last.then_inc(th0_done, 1)

            def queries(j, g, p):
                pe.wait_ge(h0T_ready, g + 1)
                at_least(pe, o_ready, g - 1)
                features(0, KC)

            def features(m0, m1_):
                for m in range(m0, m1_):
                    for k in range(KC):
                        for a, b in PAIR:
                            last = mm(bankD[:, m * TOK:(m + 1) * TOK], wt["qkv"][:, a, k, m * P:(m + 1) * P], h0T[:, b, k],
                                      k == 0 and a == 0 and b == 0)
                return last

            def keys(j, g, p):
                features(KC, 2 * KC).then_inc(qk_done, 1)

            def values(j, g, p):
                at_least(pe, pT_ready, g)
                for k in range(KC):
                    for a, b in PAIR:
                        last = mm(v_ps, h0T[:, a, k], wt["qkv"][:, b, k, 2 * D:], k == 0 and a == 0 and b == 0)
                last.then_inc(v_done, 1)

            def scores(c):
                def stage(j, g, p):
                    if c == 0:
                        pe.wait_ge(qx_ready, g + 1)
                        at_least(pe, r1_ready, g - 1)
                    for b in range(B):
                        t = slice(b * S, (b + 1) * S)
                        for x, y in PAIR:
                            last = mm(s_ps[:, c * TOK + b * S:c * TOK + (b + 1) * S], qx[:, x, c, b::B], kT[:, y, c, t],
                                      x == 0 and y == 0)
                    if c == KC - 1:
                        last.then_inc(s_done, 1)
                return stage

            def transpose_p(j, g, p):
                pe.wait_ge(e_split, g + 1)
                at_least(pe, h0T_ready, upto(g + 2))
                at_least(pe, h1T_ready, g - 1)
                for a in range(2):
                    for c in range(KC):
                        last = nc.tensor.transpose(th_ps[:, 0, a, c], ehl[:, a, c * TOK:(c + 1) * TOK], eye16[:])
                last.then_inc(tp_done, 1)

            def attend(c):
                def stage(j, g, p):
                    if c == 0:
                        pe.wait_ge(px_ready, g + 1)
                        pe.wait_ge(v_ready, g + 1)
                        pe.wait_ge(qk_lo, upto(g + 2))
                    for h in range(HC):
                        for x, y in PAIR:
                            last = mm(pv_ps[:, c * HC + h], px[:, x, c, h::HC], v[:, p, y, c * HC + h],
                                      x == 0 and y == 0)
                    if c == KC - 1:
                        last.then_inc(pv_done, 1)
                return stage

            def transpose_o(j, g, p):
                pe.wait_ge(o_split, g + 1)
                pe.wait_ge(sc_ready, upto(g + 2))
                for a in range(2):
                    for c in range(KC):
                        last = nc.tensor.transpose(to_ps[:, a, c], ohl[:, a, c * P:(c + 1) * P], eye16[:])
                last.then_inc(to_done, 1)

            def project_out(j, g, p):
                pe.wait_ge(oT_ready, g + 1)
                for k in range(KC):
                    for a, b in PAIR:
                        last = mm(wo_ps, oT[:, a, k], wt["out"][:, b, k], k == 0 and a == 0 and b == 0)
                last.then_inc(wo_done, 1)

            def transpose_h1(j, g, p):
                pe.wait_ge(h1_split, g + 1)
                pe.wait_ge(v_ready, upto(g + 3))
                for a in range(2):
                    for c in range(KC):
                        last = nc.tensor.transpose(th_ps[:, 1, a, c], h1hl[:, a, c * P:(c + 1) * P], eye16[:])
                last.then_inc(th1_done, 1)

            h1v = h1T[:].rearrange("p (a c t) -> p a c t", a=2, c=KC)

            def gate_inputs(lo, hi):
                def stage(j, g, p):
                    if lo == 0:
                        pe.wait_ge(h1T_ready, g + 1)
                    for n in range(lo, hi):
                        c, m = divmod(n, NG)
                        o = gsum[p][c][:, 0:B * NG * S].rearrange("p (u m s) -> p u m s", u=B, m=NG)[:, :, m]
                        mm(o, bias2[:, D + n * P:D + (n + 1) * P], ones2[:], m == 0)
                        for k in range(KC):
                            for a, b in PAIR:
                                last = mm(o, wt["gx"][:, a, k, n * P:(n + 1) * P], h1v[:, b, k], False)
                    if hi == KC * NG:
                        last.then_inc(xp_done, 1)
                return stage

            stages = (*((k, gate_inputs(*run)) for k, run in XP.items()), (K_TH1, transpose_h1), (K_WO, project_out),
                      (K_TO, transpose_o), (K_PV0, attend(0)), (K_PV1, attend(1)), (K_TP, transpose_p),
                      (K_S0, scores(0)), (K_S1, scores(1)), (K_V, values), (K_K, keys), (K_Q, queries),
                      (K_TH0, transpose_h0), *((k, embed(*run)) for k, run in EMB.items()))

            def scan_step(j, q):
                par, u = q // B, q % B
                t = j * SLOTS + q

                def add(c, k, low):
                    for m in range(NG):
                        o = gsum[par][c][:, (u * NG + m) * S:(u * NG + m + 1) * S]
                        cols = slice((c * NG + m) * P, (c * NG + m + 1) * P)
                        if low:
                            last = mm(o, wt["gu"][:, 0, k, cols], slo[:, k], False)
                        else:
                            mm(o, wt["gu"][:, 0, k, cols], shi[:, k], False)
                            last = mm(o, wt["gu"][:, 1, k, cols], shi[:, k], False)
                    return last

                pe.wait_ge(s_hi[0], t + 1)
                add(0, 0, False)
                at_least(pe, gates[1], t)
                add(1, 0, False)
                pe.wait_ge(s_lo[0], t + 1)
                add(0, 0, True)
                add(1, 0, True)
                pe.wait_ge(s_hi[1], t + 1)
                add(0, 1, False)
                pe.wait_ge(s_lo[1], t + 1)
                add(0, 1, True).then_inc(pre[0], 1)
                add(1, 1, False)
                add(1, 1, True).then_inc(pre[1], 1)

            def slot(j, q):
                if not isinstance(j, int) or j >= 0:
                    scan_step(j, q)
                if isinstance(j, int):
                    filling(SLOTS * j + K_SCAN + q)
                for k, stage in stages:
                    at = group_of(j, q, k)
                    if at is not None:
                        stage(j, *at)

            run_slots(pe, slot)

            weights("ou")
            pe.wait_ge(cx_ready, 2)
            for k in range(KC):
                for a, b in PAIR:
                    mm(bankA[:, 0:D], cx[:, a, k], wt["ou"][:, b, k], k == 0 and a == 0 and b == 0)
            mm(bankA[:, 0:D], ones2[:], bias2[:, D + NG * D:], False).then_inc(y_done, 1)
            weights("ox")
            pe.wait_ge(h1T_kept, 16 * G)
            hk = h1Tall[:].rearrange("p (g a c t) -> p g a c t", g=G, a=2, c=KC)
            for i in range(2):
                pe.wait_ge(gates[i], G * B)
            for g in range(G):
                o = tail_banks[g % 4][:, 0:D]
                at_least(pe, t_ready, g - 3)
                for k in range(KC):
                    for a, b in PAIR:
                        mm(o, hk[:, g, a, k], wt["ox"][:, b, k], k == 0 and a == 0 and b == 0)
                if g == 0:
                    pe.wait_ge(y_split, 1)
                mm(o, eyew[:], yhl[:, 0], False)
                mm(o, eyew[:], yhl[:, 1], False).then_inc(o2_done, 1)

        @block.vector
        def _(dve):
            def weight_lo(n):
                for i, (part, scale) in enumerate(scaled(n)):
                    dve.wait_ge(w_hi[n], i + 1)
                    nc.vector.scalar_tensor_tensor(part(whl[n][:, 1]), part(w32[n][:]), scale, part(whl[n][:, 0]),
                                                   ALU.mult, ALU.subtract).then_inc(w_lo[n], 1)

            def prepare(T):
                if T == K_XHI_A:
                    nc.vector.memset(ones2[:], 1.0).then_inc(const_set, 1)
                    nc.vector.memset(minus_half[:], -0.5).then_inc(const_set, 1)
                    nc.vector.memset(eps[:], EPS).then_inc(const_set, 1)
                    nc.vector.memset(v[:, :, 0], 1.0).then_inc(const_set, 1)
                    nc.vector.memset(v[:, :, 1], 0.0).then_inc(const_set, 1)
                    dve.wait_ge(pos_m1, 1)
                    nc.vector.tensor_copy(m1[:], bankB[0:TAPS, 0:H].unsqueeze(2).broadcast_to([TAPS, H, S])).then_inc(pos_m1x, 1)
                    for i, (lo, hi, scale) in enumerate(bias_parts):
                        dve.wait_ge(b_hi, i + 1)
                        nc.vector.scalar_tensor_tensor(brow_lo[:, lo:hi], brow32[:, lo:hi], scale, bias2[0:1, lo:hi],
                                                       ALU.mult, ALU.subtract).then_inc(b_lo, 1)
                    dve.wait_ge(pos_e, 1)
                    nc.vector.tensor_copy(ed[:].rearrange("p c d -> p (c d)"), bankB[:, 0:KC * S]).then_inc(pos_ex, 1)
                    dve.wait_ge(pos_ex, 1)
                    for c in range(KC):
                        bc = inc_sb[:, c:c + 1].broadcast_to([P, S])
                        nc.vector.tensor_scalar(shi[:, c], bc, 2.0, None, ALU.mult).then_inc(s_hi[c], 1)
                        nc.vector.tensor_scalar(s32[:, c], bc, 2.0, None, ALU.mult).then_inc(s_32[c], 1)
                        dve.wait_ge(s_32[c], 1)
                        nc.vector.tensor_tensor(slo[:, c], s32[:, c], shi[:, c], ALU.subtract).then_inc(s_lo[c], 1)
                if T == 1:
                    for c in range(KC):
                        at_least(dve, pos_set, c)
                        nc.vector.tensor_tensor(picked[:], pick_sb[:], ed[:, c].unsqueeze(1).broadcast_to([P, S, S]),
                                                ALU.mult).then_inc(pos_pick, 1)
                        dve.wait_ge(pos_pick, c + 1)
                        nc.vector.reduce_sum(posb[:, c], picked[:], AX_X).then_inc(pos_set, 1)
                for k, n in ((K_XHI_A, "tok"), (3, "qkv"), (K_VOUT, "out"), (20, "gx"), (22, "gu"), (24, "ox"), (25, "ou")):
                    if T == k:
                        weight_lo(n)

            def qk_pair_lo(j, g, p):
                dve.wait_ge(qk_hi, g + 1)
                for c in range(KC):
                    nc.vector.scalar_tensor_tensor(qT[:, 1, c].rearrange("p s b -> p b s"),
                                                   q_ps[:, c * TOK:(c + 1) * TOK].rearrange("p (b s) -> p b s", b=B),
                                                   UNSCALE, qT[:, 0, c].rearrange("p s b -> p b s"),
                                                   ALU.mult, ALU.subtract)
                nc.vector.scalar_tensor_tensor(kT[:, 1].rearrange("p c t -> p (c t)"), k_ps, UNSCALE,
                                               kT[:, 0].rearrange("p c t -> p (c t)"),
                                               ALU.mult, ALU.subtract).then_inc(qk_lo, 1)

            def spread_q(run):
                def stage(j, g, p):
                    if run == 0:
                        dve.wait_ge(qk_lo, g + 1)
                    for h in range(*QX_RUNS[run]):
                        last = nc.vector.tensor_scalar(qx[:, :, :, h * TOK:(h + 1) * TOK], qT[:].rearrange("p a c s b -> p a c (s b)"),
                                                       block_sb[:, h:h + 1], None, ALU.mult)
                    if run == 1:
                        last.then_inc(qx_ready, 1)
                return stage

            def spread_p(run):
                def stage(j, g, p):
                    if run == 0:
                        dve.wait_ge(pT_ready, g + 1)
                    for b in range(*PX_RUNS[run]):
                        last = nc.vector.tensor_scalar(px[:, :, :, b * P:(b + 1) * P], pT[:].rearrange("p a c s h -> p a c (s h)"),
                                                       block_sb[:, b:b + 1], None, ALU.mult)
                    if run == 1:
                        last.then_inc(px_ready, 1)
                return stage

            def v_pair_lo(j, g, p):
                dve.wait_ge(v_hi, g + 1)
                nc.vector.scalar_tensor_tensor(v[:, p, 1, :, 0:HD], v_ps.rearrange("p (h w) -> p h w", w=HD), UNSCALE,
                                               v[:, p, 0, :, 0:HD], ALU.mult, ALU.subtract).then_inc(v_ready, 1)

            def softmax_shift(j, g, p):
                dve.wait_ge(s_done, g + 1)
                if isinstance(g, int) and g == 0:
                    dve.wait_ge(pos_set, KC)
                for c in range(KC):
                    last = nc.vector.tensor_tensor(sc[:, c], s_ps.rearrange("p (c b j) -> p c b j", c=KC, b=B)[:, c],
                                                   posb[:, c].unsqueeze(1).broadcast_to([P, B, S]), ALU.add)
                last.then_inc(sc_ready, 1)
                dve.wait_ge(sc_ready, g + 1)
                nc.vector.reduce_max(mx[:], sc[:], AX_X).then_inc(mx_ready, 1)
                dve.wait_ge(mx_ready, g + 1)
                at_least(dve, e_ready, g)
                nc.vector.tensor_tensor(scm[:], sc[:], mx[:].unsqueeze(3).broadcast_to([P, KC, B, S]),
                                        ALU.subtract).then_inc(scm_ready, 1)

            def divide_sum(j, g, p):
                dve.wait_ge(pv_done, g + 1)
                nc.vector.reciprocal(rs[:], pv_ps[:, :, HD]).then_inc(rs_ready, 1)
                dve.wait_ge(rs_ready, g + 1)
                at_least(dve, o_split, g)
                nc.vector.tensor_tensor(o32[:].rearrange("p (h w) -> p h w", w=HD), pv_ps[:, :, 0:HD],
                                        rs[:].unsqueeze(2).broadcast_to([P, H, HD]), ALU.mult).then_inc(o_ready, 1)

            def residual_stats(j, g, p):
                h = hall[:, bass.ds(g * D, D)]
                dve.wait_ge(wo_done, g + 1)
                nc.vector.scalar_tensor_tensor(r1[:], wo_ps, UNSCALE, h, ALU.mult, ALU.add).then_inc(r1_ready, 1)
                dve.wait_ge(r1_ready, g + 1)
                nc.vector.bn_stats(stats[:], r1[:]).then_inc(st1_ready, 1)
                dve.wait_ge(st1_ready, g + 1)
                dve.sem_inc(st1_seen, 1)
                nc.vector.bn_aggr(mv[:], stats[:]).then_inc(mv1_ready, 1)

            def first_norm(j, g, p):
                h = hall[:, bass.ds(g * D, D)]
                dve.wait_ge(rstd1_ready, g + 1)
                nc.vector.tensor_scalar(h, r1[:], mv[:, 0:1], rstd[:], ALU.subtract, ALU.mult).then_inc(h1_ready, 1)

            stages = ((K_H1, first_norm), (K_LN, residual_stats), (K_O, divide_sum), (K_SM, softmax_shift),
                      (K_VOUT, v_pair_lo),
                      (K_PX[0], spread_p(0)), (K_PX[1], spread_p(1)), (K_QK, qk_pair_lo), (K_QX[0], spread_q(0)),
                      (K_QX[1], spread_q(1)))

            def scan_state(j, q):
                t = j * SLOTS + (q + 1)

                def addend(c):
                    dve.wait_ge(gates[c], t)
                    nc.vector.scalar_tensor_tensor(keepf[:, c], gate[:, c, 0:S], 1.0, s32[:, c], ALU.add, ALU.mult)
                    nc.vector.scalar_tensor_tensor(inp[:, c], gate[:, c, S:2 * S], 1.0, gate[:, c, 2 * S:3 * S],
                                                   ALU.add, ALU.mult).then_inc(addends[c], 1)

                def total(c):
                    dve.wait_ge(addends[c], t)
                    nc.vector.scalar_tensor_tensor(shi[:, c], keepf[:, c], 0.5, inp[:, c], ALU.mult, ALU.add).then_inc(s_hi[c], 1)
                    nc.vector.scalar_tensor_tensor(s32[:, c], keepf[:, c], 0.5, inp[:, c], ALU.mult, ALU.add).then_inc(s_32[c], 1)

                def low(c):
                    dve.wait_ge(s_32[c], t + 1)
                    nc.vector.tensor_tensor(slo[:, c], s32[:, c], shi[:, c], ALU.subtract).then_inc(s_lo[c], 1)

                addend(0)
                total(0)
                addend(1)
                low(0)
                total(1)
                low(1)

            def slot(j, q):
                if not isinstance(j, int) or j >= 0:
                    scan_state(j, q)
                if isinstance(j, int):
                    prepare(SLOTS * j + K_SCAN + q)
                for k, stage in stages:
                    at = group_of(j, q, k)
                    if at is not None:
                        stage(j, *at)

            run_slots(dve, slot)

            n = G * B + 1
            for c in range(KC):
                dve.wait_ge(s_lo[c], n)
            for a, s_ in ((0, shi), (1, slo)):
                nc.vector.tensor_copy(cx[:, a], s_[:].unsqueeze(2).broadcast_to([P, KC, B, S])).then_inc(cx_ready, 1)

            def finish(g):
                i = g % 4
                dve.wait_ge(rstd2_ready, g + 1)
                if g >= 4:
                    dve.wait_ge(out_in[i], 16 * (g // 4))
                nc.vector.tensor_scalar(res[:, i], r2[:, i], mv2[:, i, 0:1], rstd2[:, i:i + 1], ALU.subtract,
                                        ALU.mult).then_inc(res_ready, 1)

            for g in range(G):
                i = g % 4
                dve.wait_ge(t_ready, g + 1)
                nc.vector.tensor_tensor(r2[:, i], t32[:, i], hall[:, g * D:(g + 1) * D], ALU.add).then_inc(r2_ready, 1)
                dve.wait_ge(r2_ready, g + 1)
                nc.vector.bn_stats(stats2[:, i], r2[:, i]).then_inc(st2_ready, 1)
                dve.wait_ge(st2_ready, g + 1)
                nc.vector.bn_aggr(mv2[:, i], stats2[:, i]).then_inc(mv2_ready, 1)
                if g >= 2:
                    finish(g - 2)
            finish(G - 2)
            finish(G - 1)

        @block.gpsimd
        def _(pool):
            def x_pair_lo(half):
                def stage(j, g, p):
                    pool.wait_ge(x_hi, g * 2 + (half + 1))
                    c = slice(half * PC // 2, (half + 1) * PC // 2)
                    nc.gpsimd.tensor_tensor(xhl[:, 1, c], x32[:, p, c], xhl[:, 0, c], ALU.subtract).then_inc(x_split, 1)
                return stage

            def h0_pair_lo(j, g, p):
                pool.wait_ge(h0_ready, g + 1)
                nc.gpsimd.tensor_tensor(h0hl[:, 1], hall[:, bass.ds(g * D, D)], h0hl[:, 0], ALU.subtract).then_inc(h0_split, 1)

            def e_pair_lo(j, g, p):
                pool.wait_ge(e_hi, g + 1)
                nc.gpsimd.tensor_tensor(ehl[:, 1], e32[:], ehl[:, 0], ALU.subtract).then_inc(e_split, 1)

            def o_pair_lo(j, g, p):
                pool.wait_ge(o_hi, g + 1)
                nc.gpsimd.tensor_tensor(ohl[:, 1], o32[:], ohl[:, 0], ALU.subtract).then_inc(o_split, 1)

            def rstd1(j, g, p):
                pool.wait_ge(mv1_ready, g + 1)
                nc.gpsimd.tensor_tensor(veps[:], mv[:, 1:2], eps[:], ALU.add).then_inc(ve1_ready, 1)
                pool.wait_ge(ve1_ready, g + 1)
                nc.gpsimd.tensor_tensor(rstd[:], veps[:], minus_half[:], ALU.pow).then_inc(rstd1_ready, 1)

            def h1_pair_lo(j, g, p):
                pool.wait_ge(h1_hi, g + 1)
                nc.gpsimd.tensor_tensor(h1hl[:, 1], hall[:, bass.ds(g * D, D)], h1hl[:, 0], ALU.subtract).then_inc(h1_split, 1)

            pool.wait_ge(const_set, 3)

            stages = ((K_H1HL, h1_pair_lo), (K_LN, rstd1), (K_OHL, o_pair_lo), (K_EXP, e_pair_lo), (K_H0, h0_pair_lo),
                      (K_XHI_A, x_pair_lo(0)), (K_XHI_B, x_pair_lo(1)))

            def slot(j, q):
                for k, stage in stages:
                    at = group_of(j, q, k)
                    if at is not None:
                        stage(j, *at)

            run_slots(pool, slot)

            pool.wait_ge(y_hi, 1)
            nc.gpsimd.tensor_tensor(yhl[:, 1], y32[:], yhl[:, 0], ALU.subtract).then_inc(y_split, 1)
            for g in range(G):
                i = g % 4
                pool.wait_ge(mv2_ready, g + 1)
                nc.gpsimd.tensor_scalar(veps2[:, i:i + 1], mv2[:, i, 1:2], EPS, None, ALU.add).then_inc(ve2_ready, 1)
                pool.wait_ge(ve2_ready, g + 1)
                nc.gpsimd.tensor_tensor(rstd2[:, i:i + 1], veps2[:, i:i + 1], minus_half[:], ALU.pow).then_inc(rstd2_ready, 1)


def kernel(x, L0_tok_W, L0_tok_b, L0_attn_Wqkv, L0_attn_Wout, L0_attn_Wpos, L0_attn_coeffs,
           L0_ffn_wf, L0_ffn_uf, L0_ffn_bf, L0_ffn_wi, L0_ffn_ui, L0_ffn_bi, L0_ffn_wc, L0_ffn_uc, L0_ffn_bc,
           L0_ffn_wo, L0_ffn_uo, L0_ffn_bo, L0_ffn_in_c):
    import numpy as np
    import concourse.bacc as bacc
    from concourse.bass_utils import run_bass_kernel_spmd

    def rows(w, chunks):
        w = np.asarray(w)
        return np.ascontiguousarray(w.T.reshape(chunks, P, w.shape[0]).transpose(1, 0, 2).reshape(P, -1))

    def gates_of(ws):
        w = np.stack([np.asarray(a) for a in ws])
        w = w.reshape(NG, KC, P, KC, P).transpose(4, 3, 1, 0, 2)
        return np.ascontiguousarray(w.reshape(P, -1))

    x = np.asarray(x)
    blocks = x.reshape(x.shape[0], 3, 4, 16, 4, 16).transpose(0, 1, 2, 4, 3, 5)
    patches = blocks.reshape(G, TOK, PC, P)
    xT = np.ascontiguousarray(patches.transpose(3, 0, 2, 1).reshape(P, -1))
    gb = np.stack([np.asarray(a) for a in (L0_ffn_bf, L0_ffn_bi, L0_ffn_bc)]).reshape(NG, KC, P).transpose(1, 0, 2)
    brow = np.concatenate([np.asarray(L0_tok_b), gb.reshape(-1), np.asarray(L0_ffn_bo)]).reshape(1, -1)

    idx = np.clip(np.round(np.arange(S, dtype=np.float32) / np.float32(S - 1) * (RES - 1)).astype(int), 0, RES - 1)
    ramp = np.linspace(0.0, 1.0, RES).astype(np.float32)
    lag = idx[None, :] - np.arange(TAPS)[:, None]
    protoT = np.where(lag >= 0, ramp[np.maximum(lag, 0)], 0).astype(np.float32)
    i, jj, d = np.meshgrid(np.arange(S), np.arange(S), np.arange(S), indexing="ij")
    pick = np.tile((np.abs(i - jj) == d).astype(np.float32).reshape(S, S * S), (HC, 1))

    blocks16 = np.repeat(np.eye(HC, dtype=np.float32), HD, axis=0)

    arrays = {
        "xT": xT, "w_tok": rows(L0_tok_W, PC), "w_qkv": rows(L0_attn_Wqkv, KC), "w_out": rows(L0_attn_Wout, KC),
        "w_gx": gates_of((L0_ffn_wf, L0_ffn_wi, L0_ffn_wc)), "w_gu": gates_of((L0_ffn_uf, L0_ffn_ui, L0_ffn_uc)),
        "w_ox": rows(L0_ffn_wo, KC), "w_ou": rows(L0_ffn_uo, KC), "brow": brow,
        "in_c": np.ascontiguousarray(np.asarray(L0_ffn_in_c).reshape(KC, P).T),
        "coeffs": np.asarray(L0_attn_coeffs), "wpos": np.ascontiguousarray(np.asarray(L0_attn_Wpos).T),
        "protoT": protoT, "pick": pick, "blocks": blocks16, "eye": np.eye(P, dtype=np.float32),
    }
    nc = bacc.Bacc("TRN2", target_bir_lowering=False, num_devices=1)
    args = {n: nc.dram_tensor(n + "_dram", a.shape, mybir.dt.from_np(a.dtype), kind="ExternalInput").ap()
            for n, a in arrays.items()}
    out = nc.dram_tensor("out_dram", (G * TOK, D), F32, kind="ExternalOutput").ap()
    vit_layer(nc, **args, out=out)
    r = run_bass_kernel_spmd(nc, [{n + "_dram": a for n, a in arrays.items()}], core_ids=[0])
    return r.results[0]["out_dram"].reshape(x.shape[0], S, D)
```

```python
from contextlib import ExitStack

import concourse.bass as bass
from concourse import mybir
from concourse.alu_op_type import AluOpType as ALU

ACT = mybir.ActivationFunctionType
F32 = mybir.dt.float32
F16 = mybir.dt.float16
AX_X = mybir.AxisListType.X

P = 128
D = 256
KC = D // P
S = 16
B = 8
TOK = B * S
G = 16
H = 16
HD = D // H
HC = H // KC
PC = 6
NG = 3
TAPS, RES, NF = 101, 128, 4
VW = HD + 1

WSCALE = 256.0
UNSCALE = 1.0 / WSCALE
EPS = 1e-5

K_XHI_A = -3
K_XHI_B = -2
EMB = {-2: (0, 1), -1: (1, 3), 0: (3, 4), 1: (4, 5), 3: (5, 6)}
K_H0 = 4
K_TH0 = 7
K_H0T = 7
QK_MM = {8: (0, 2), 9: (2, 4)}
K_QK = 10
QX = {11: (0, 4), 12: (4, 6)}
QX_ACT = {12: (6, 8)}
V_MM = {12: (0, 2)}
K_VOUT = 13
S_MM = {13: (0, 12), 14: (12, 16)}
K_SM = 15
K_EXP = 16
K_TP = 17
K_PT = 17
PX = {17: (0, 5), 18: (5, 7)}
PX_ACT = {19: (7, 8)}
PV_MM = {19: (0, 1), 20: (1, 8), 21: (8, 16)}
K_O = 22
K_OHL = 23
K_TO = 24
K_OT = 25
WO_MM = {26: (0, 2)}
K_LN = 27
K_H1 = 28
K_H1HL = 29
K_TH1 = 30
K_H1T = 30
XP = {32: (0, 1), 33: (1, 2), 35: (2, 6)}
K_SCAN = 36
SLOTS = 2 * B
PAIRS = G // 2


def at_least(eng, sem, value):
    if isinstance(value, int) and value <= 0:
        return
    eng.wait_ge(sem, value)


def upto(value):
    return min(value, G) if isinstance(value, int) else value


def run_slots(eng, slot):
    first = -((K_SCAN - K_XHI_A + SLOTS - 1) // SLOTS)
    full = PAIRS - (K_SCAN + SLOTS - 1 - K_XHI_A) // SLOTS
    for j in range(first, 0):
        for q in range(SLOTS):
            slot(j, q)
    with eng.Fori(0, full) as j:
        for q in range(SLOTS):
            slot(j, q)
    for j in range(full, PAIRS):
        for q in range(SLOTS):
            slot(j, q)


def before(k, other):
    return (k - other - 1) // B + 1


def bank_free(eng, g, k, holders):
    for slot, read in holders:
        at_least(eng, read, upto(g + before(k, slot)))


def group_of(j, q, k):
    d, r = divmod(K_SCAN + q - k, B)
    if r:
        return None
    if isinstance(j, int):
        g = 2 * j + d
        return (g, d % 2) if 0 <= g < G else None
    return (j * 2 + d, d % 2)


def vit_layer(nc, xT, w_tok, w_qkv, w_out, w_gx, w_gu, w_ox, w_ou, brow, in_c, coeffs, wpos,
              protoT, pick, blocks, eye, out):
    with ExitStack() as ctx:
        def sb(name, shape, dt):
            return ctx.enter_context(nc.sbuf_tensor(name, shape, dt))

        def bank(name):
            return ctx.enter_context(nc.psum_tensor(name, [P, 512], F32))

        def sem(name):
            return ctx.enter_context(nc.semaphore(name))

        w_shapes = {"tok": PC * D, "qkv": KC * 3 * D, "out": KC * D, "gx": KC * NG * D,
                    "gu": KC * NG * D, "ox": KC * D, "ou": KC * D}
        w_dram = {"tok": w_tok, "qkv": w_qkv, "out": w_out, "gx": w_gx, "gu": w_gu, "ox": w_ox, "ou": w_ou}
        w32 = {n: sb("w32_" + n, [P, c], F32) for n, c in w_shapes.items()}
        whl = {n: sb("whl_" + n, [P, 2, c], F16) for n, c in w_shapes.items()}
        NB = D + NG * D + D
        brow32 = sb("brow32", [1, NB], F32)
        brow_lo = sb("brow_lo", [1, NB], F16)
        bias2 = sb("bias2", [2, NB], F16)
        ones2 = sb("ones2", [2, P], F16)

        eye32 = sb("eye32", [P, P], F32)
        eye16 = sb("eye16", [P, P], F16)
        eyew = sb("eyew", [P, P], F16)
        coef_sb = sb("coef_sb", [NF, TAPS], F32)
        wpos_sb = sb("wpos_sb", [NF, H], F32)
        proto_sb = sb("proto_sb", [TAPS, S], F32)
        pick_sb = sb("pick_sb", [P, S, S], F32)
        m1 = sb("m1", [TAPS, H, S], F32)
        ed = sb("ed", [P, KC, S], F32)
        picked = sb("picked", [P, S, S], F32)
        posb = sb("posb", [P, KC, S], F32)
        block_sb = sb("block_sb", [P, HC], F32)
        minus_half = sb("minus_half", [P, 1], F32)
        eps = sb("eps", [P, 1], F32)

        x32 = sb("x32", [P, 2, PC, TOK], F32)
        xhl = sb("xhl", [P, 2, PC, TOK], F16)
        hall = sb("hall", [P, G * D], F32)
        h0hl = sb("h0hl", [P, 2, D], F16)
        h0T = sb("h0T", [P, 2, KC, TOK], F16)
        qT = sb("qT", [P, 2, KC, S, B], F16)
        kT = sb("kT", [P, 2, KC, TOK], F16)
        v = sb("v", [P, 2, 2, H, VW], F16)
        qx = sb("qx", [P, 2, KC, HC * S * B], F16)
        sc = sb("sc", [P, KC, B, S], F32)
        mx = sb("mx", [P, KC, B], F32)
        scm = sb("scm", [P, KC, B, S], F32)
        e32 = sb("e32", [P, KC * TOK], F32)
        ehl = sb("ehl", [P, 2, KC * TOK], F16)
        pT = sb("pT", [P, 2, KC, S, HC], F16)
        px = sb("px", [P, 2, KC, B * S * HC], F16)
        rs = sb("rs", [P, H], F32)
        o32 = sb("o32", [P, D], F32)
        ohl = sb("ohl", [P, 2, D], F16)
        oT = sb("oT", [P, 2, KC, TOK], F16)
        r1 = sb("r1", [P, D], F32)
        stats = sb("stats", [P, 6], F32)
        mv = sb("mv", [P, 2], F32)
        veps = sb("veps", [P, 1], F32)
        rstd = sb("rstd", [P, 1], F32)
        h1hl = sb("h1hl", [P, 2, D], F16)
        h1T = sb("h1T", [P, 2 * KC * TOK], F16)
        h1Tall = sb("h1Tall", [P, G * 2 * KC * TOK], F16)

        inc_sb = sb("inc_sb", [P, KC], F32)
        s32 = sb("s32", [P, KC, S], F32)
        shi = sb("shi", [P, KC, S], F16)
        slo = sb("slo", [P, KC, S], F16)
        gate = sb("gate", [P, KC, NG * S], F32)
        keepf = sb("keepf", [P, KC, S], F32)
        inp = sb("inp", [P, KC, S], F32)

        cx = sb("cx", [P, 2, KC, B, S], F16)
        y32 = sb("y32", [P, D], F32)
        yhl = sb("yhl", [P, 2, D], F16)
        t32 = sb("t32", [P, 4, D], F32)
        r2 = sb("r2", [P, 4, D], F32)
        res = sb("res", [P, 4, D], F32)
        stats2 = sb("stats2", [P, 4, 6], F32)
        mv2 = sb("mv2", [P, 4, 2], F32)
        veps2 = sb("veps2", [P, 4], F32)
        rstd2 = sb("rstd2", [P, 4], F32)

        gsum2 = [ctx.enter_context(nc.psum_tensor(f"gsum{p}", [P, KC * 512], F32)) for p in range(2)]
        gsum = [[t[:, c * 512:(c + 1) * 512] for c in range(KC)] for t in gsum2]
        bankA, bankB, bankC, bankD = bank("bankA"), bank("bankB"), bank("bankC"), bank("bankD")
        tail_banks = gsum[0] + gsum[1]
        emb_ps = bankA[:, 0:D]
        s_ps = bankB[:, 0:KC * TOK]
        to_ps = bankB[:].bitcast(F16)[:, 0:512].rearrange("p (a c t) -> p a c t", a=2, c=KC)
        wo_ps = bankB[:, 0:D]
        th_ps = bankC[:].bitcast(F16).rearrange("p (w a c t) -> p w a c t", w=2, a=2, c=KC)
        v_ps = bankC[:, 0:D]
        q_ps, k_ps = bankD[:, 0:KC * TOK], bankD[:, KC * TOK:]
        pv_ps = bankD[:, 0:H * VW].rearrange("p (h w) -> p h w", w=VW)

        w_in = {n: sem("w_in_" + n) for n in w_shapes}
        small_in = sem("small_in")
        w_hi = {n: sem("w_hi_" + n) for n in w_shapes}
        w_lo = {n: sem("w_lo_" + n) for n in w_shapes}
        const_set, eye_set = sem("const_set"), sem("eye_set")
        b_hi, b_lo, b_row = sem("b_hi"), sem("b_lo"), sem("b_row")
        pos_m1, pos_m1x, pos_e, pos_ex, pos_pick, pos_set = (
            sem("pos_m1"), sem("pos_m1x"), sem("pos_e"), sem("pos_ex"), sem("pos_pick"), sem("pos_set"))
        x_in = [sem("x_in0"), sem("x_in1")]
        x_hi, x_split = sem("x_hi"), sem("x_split")
        emb_done, h0_ready, h0_split = sem("emb_done"), sem("h0_ready"), sem("h0_split")
        th0_done, h0T_ready = sem("th0_done"), sem("h0T_ready")
        qk_done, qk_hi, qk_lo, qx_ready = sem("qk_done"), sem("qk_hi"), sem("qk_lo"), sem("qx_ready")
        v_done, v_hi, v_ready = sem("v_done"), sem("v_hi"), sem("v_ready")
        s_done, sc_ready, mx_ready, scm_ready = sem("s_done"), sem("sc_ready"), sem("mx_ready"), sem("scm_ready")
        e_ready, e_hi, e_split = sem("e_ready"), sem("e_hi"), sem("e_split")
        tp_done, pT_ready, px_ready = sem("tp_done"), sem("pT_ready"), sem("px_ready")
        pv_done, rs_ready, o_ready, o_hi, o_split = (
            sem("pv_done"), sem("rs_ready"), sem("o_ready"), sem("o_hi"), sem("o_split"))
        to_done, oT_ready = sem("to_done"), sem("oT_ready")
        wo_done, r1_ready, st1_ready, st1_seen, mv1_ready, ve1_ready, rstd1_ready = (
            sem("wo_done"), sem("r1_ready"), sem("st1_ready"), sem("st1_seen"), sem("mv1_ready"), sem("ve1_ready"),
            sem("rstd1_ready"))
        h1_ready, h1_hi, h1_split = sem("h1_ready"), sem("h1_hi"), sem("h1_split")
        th1_done, h1T_ready, h1T_kept, xp_done = (
            sem("th1_done"), sem("h1T_ready"), sem("h1T_kept"), sem("xp_done"))
        pre, gates, addends = sem("pre"), sem("gates"), sem("addends")
        s_hi, s_32, s_lo = sem("s_hi"), sem("s_32"), sem("s_lo")
        cx_ready, y_done, y_ready, y_hi, y_split = (
            sem("cx_ready"), sem("y_done"), sem("y_ready"), sem("y_hi"), sem("y_split"))
        o2_done, t_ready, r2_ready, st2_ready, mv2_ready, ve2_ready, rstd2_ready, res_ready = (
            sem("o2_done"), sem("t_ready"), sem("r2_ready"), sem("st2_ready"), sem("mv2_ready"),
            sem("ve2_ready"), sem("rstd2_ready"), sem("res_ready"))
        out_in = [sem(f"out_in{i}") for i in range(4)]

        qx_act, px_act = sem("qx_act"), sem("px_act")
        bankB_use = ((min(S_MM), sc_ready), (K_TO, oT_ready), (min(WO_MM), r1_ready))
        bankC_use = ((K_TH0, h0T_ready), (min(V_MM), v_ready), (K_TP, pT_ready), (K_TH1, h1T_ready))
        bankD_use = ((min(QK_MM), qk_lo), (min(PV_MM), o_ready))
        q_flat = qT[:].rearrange("p a c s b -> p a c (s b)")
        p_flat = pT[:].rearrange("p a c s h -> p a c (s h)")

        def q_wait(eng, g):
            eng.wait_ge(qk_lo, g + 1)

        def p_wait(eng, g):
            eng.wait_ge(pT_ready, g + 1)

        block = ctx.enter_context(nc.Block())

        def scaled(n):
            if n == "qkv":
                w = lambda t: t.rearrange("p (k e) -> p k e", k=KC)
                return [(lambda t: w(t)[:, :, 0:D], WSCALE * HD ** -0.5), (lambda t: w(t)[:, :, D:3 * D], WSCALE)]
            if n in ("gx", "gu"):
                f = 1.0 if n == "gx" else 0.5
                w = lambda t: t.rearrange("p (k e) -> p k e", e=NG * P)
                return [(lambda t: w(t)[:, :, 0:2 * P], WSCALE * 0.5 * f), (lambda t: w(t)[:, :, 2 * P:], WSCALE * f)]
            return [(lambda t: t, WSCALE * (0.5 if n == "ou" else 1.0))]

        bias_parts = [(0, D, WSCALE)]
        for c in range(KC):
            o = D + c * NG * P
            bias_parts += [(o, o + 2 * P, WSCALE * 0.5), (o + 2 * P, o + 3 * P, WSCALE)]
        bias_parts += [(D + NG * D, NB, WSCALE)]

        @block.sync
        def _(sp):
            xg = xT.rearrange("p (g c) -> p g c", g=G)
            sp.dma_start(x32[:, 0].rearrange("p c t -> p (c t)"), xg[:, 0, :]).then_inc(x_in[0], 16)
            sp.dma_start(w32["tok"][:], w_tok).then_inc(w_in["tok"], 16)
            for t, a in ((brow32, brow), (eye32, eye), (coef_sb, coeffs), (wpos_sb, wpos), (proto_sb, protoT),
                         (inc_sb, in_c), (block_sb, blocks)):
                sp.dma_start(t[:], a).then_inc(small_in, 16)
            sp.dma_start(pick_sb[:].rearrange("p j d -> p (j d)"), pick).then_inc(small_in, 16)
            for n in ("qkv", "out", "gx", "gu", "ox", "ou"):
                sp.dma_start(w32[n][:], w_dram[n]).then_inc(w_in[n], 16)
            sp.wait_ge(b_lo, len(bias_parts))
            sp.dma_start(bias2[1:2, :], brow_lo[:]).then_inc(b_row, 16)

            def load_x(j, g, p):
                at_least(sp, x_split, g * 2 - 2)
                sp.dma_start(x32[:, p].rearrange("p c t -> p (c t)"),
                             xT[:, bass.ds(g * (PC * TOK), PC * TOK)]).then_inc(x_in[p], 16)

            def keep_h1T(j, g, p):
                sp.wait_ge(h1T_ready, g + 1)
                w = 2 * KC * TOK
                sp.dma_start(h1Tall[:, bass.ds(g * w, w)], h1T[:]).then_inc(h1T_kept, 16)

            def slot(j, q):
                for k, stage in ((K_H1T, keep_h1T), (-B, load_x)):
                    at = group_of(j, q, k)
                    if at is None or (stage is load_x and isinstance(at[0], int) and at[0] == 0):
                        continue
                    stage(j, *at)

            run_slots(sp, slot)

            for g in range(G):
                sp.wait_ge(res_ready, g + 1)
                sp.dma_start(out[g * TOK:(g + 1) * TOK, :], res[:, g % 4]).then_inc(out_in[g % 4], 16)
            for i in range(4):
                sp.wait_ge(out_in[i], 16 * (G // 4))

        @block.scalar
        def _(act):
            def weight_hi(n):
                act.wait_ge(w_in[n], 16)
                for part, scale in scaled(n):
                    nc.scalar.activation(part(whl[n][:, 0]), part(w32[n][:]), ACT.Copy, scale=scale).then_inc(w_hi[n], 1)

            def prepare(T):
                if T == K_XHI_A:
                    act.wait_ge(small_in, 16 * 8)
                    for lo, hi, scale in bias_parts:
                        nc.scalar.activation(bias2[0:1, lo:hi], brow32[:, lo:hi], ACT.Copy, scale=scale).then_inc(b_hi, 1)
                    nc.scalar.activation(eye16[:], eye32[:], ACT.Copy).then_inc(eye_set, 1)
                    nc.scalar.activation(eyew[:], eye32[:], ACT.Copy, scale=WSCALE).then_inc(eye_set, 1)
                for k, n in ((K_XHI_A, "tok"), (3, "qkv"), (14, "out"), (20, "gx"), (22, "gu"), (24, "ox"), (25, "ou")):
                    if T == k:
                        weight_hi(n)

            def x_pair_hi(half):
                def stage(j, g, p):
                    if half == 0:
                        act.wait_ge(x_in[p], g * 8 + (16 - 8 * p))
                    at_least(act, emb_done, g)
                    c = slice(half * PC // 2, (half + 1) * PC // 2)
                    nc.scalar.activation(xhl[:, 0, c], x32[:, p, c], ACT.Copy).then_inc(x_hi, 1)
                return stage

            def h0_out(j, g, p):
                act.wait_ge(emb_done, g + 1)
                at_least(act, th0_done, g)
                nc.scalar.activation(hall[:, bass.ds(g * D, D)], emb_ps, ACT.Copy, scale=UNSCALE)
                nc.scalar.activation(h0hl[:, 0], emb_ps, ACT.Copy, scale=UNSCALE).then_inc(h0_ready, 1)

            def h0T_out(j, g, p):
                act.wait_ge(th0_done, g + 1)
                at_least(act, v_done, g)
                nc.scalar.activation(h0T[:], th_ps[:, 0], ACT.Copy).then_inc(h0T_ready, 1)

            def qk_out(j, g, p):
                act.wait_ge(qk_done, g + 1)
                at_least(act, s_done, g)
                nc.scalar.activation(kT[:, 0], k_ps.rearrange("p (c t) -> p c t", c=KC), ACT.Copy, scale=UNSCALE)
                nc.scalar.activation(qT[:, 0].rearrange("p c s b -> p c b s"),
                                     q_ps.rearrange("p (c b s) -> p c b s", c=KC, b=B), ACT.Copy,
                                     scale=UNSCALE).then_inc(qk_hi, 1)

            def spread(dst, src, heads, waits, done):
                def stage(j, g, p):
                    waits(act, g)
                    for h in range(*heads):
                        last = nc.scalar.activation(dst[:, :, :, h * P:(h + 1) * P], src, ACT.Copy, scale=block_sb[:, h:h + 1])
                    last.then_inc(done, 1)
                return stage

            def v_out(j, g, p):
                act.wait_ge(v_done, g + 1)
                at_least(act, pv_done, g - 1)
                nc.scalar.activation(v[:, p, 0, :, 0:HD], v_ps.rearrange("p (h w) -> p h w", w=HD), ACT.Copy,
                                     scale=UNSCALE).then_inc(v_hi, 1)

            def exponential(j, g, p):
                act.wait_ge(scm_ready, g + 1)
                at_least(act, e_split, g)
                nc.scalar.activation(e32[:], scm[:].rearrange("p c b j -> p (c b j)"), ACT.Exp).then_inc(e_ready, 1)
                act.wait_ge(e_ready, g + 1)
                at_least(act, tp_done, g)
                nc.scalar.activation(ehl[:, 0], e32[:], ACT.Copy).then_inc(e_hi, 1)

            def pT_out(j, g, p):
                act.wait_ge(tp_done, g + 1)
                at_least(act, pv_done, g)
                nc.scalar.activation(pT[:].rearrange("p a c s h -> p (a c) h s"),
                                     th_ps[:, 0].rearrange("p a c (h s) -> p (a c) h s", h=HC), ACT.Copy).then_inc(pT_ready, 1)

            def o_pair_hi(j, g, p):
                act.wait_ge(o_ready, g + 1)
                at_least(act, to_done, g)
                nc.scalar.activation(ohl[:, 0], o32[:], ACT.Copy).then_inc(o_hi, 1)

            def oT_out(j, g, p):
                act.wait_ge(to_done, g + 1)
                at_least(act, wo_done, g)
                nc.scalar.activation(oT[:], to_ps, ACT.Copy).then_inc(oT_ready, 1)

            def h1_pair_hi(j, g, p):
                act.wait_ge(h1_ready, g + 1)
                at_least(act, th1_done, g)
                nc.scalar.activation(h1hl[:, 0], hall[:, bass.ds(g * D, D)], ACT.Copy).then_inc(h1_hi, 1)

            def h1T_out(j, g, p):
                act.wait_ge(th1_done, g + 1)
                at_least(act, xp_done, g)
                at_least(act, h1T_kept, g * 16)
                nc.scalar.activation(h1T[:], th_ps[:, 1].rearrange("p a c t -> p (a c t)"), ACT.Copy).then_inc(h1T_ready, 1)

            stages = (*((k, spread(qx, q_flat, run, q_wait, qx_act)) for k, run in QX_ACT.items()),
                      *((k, spread(px, p_flat, run, p_wait, px_act)) for k, run in PX_ACT.items()),
                      (K_H1T, h1T_out), (K_H1HL, h1_pair_hi), (K_OT, oT_out), (K_OHL, o_pair_hi), (K_PT, pT_out),
                      (K_EXP, exponential), (K_VOUT, v_out), (K_QK, qk_out), (K_H0T, h0T_out), (K_H0, h0_out),
                      (K_XHI_A, x_pair_hi(0)), (K_XHI_B, x_pair_hi(1)))

            def slot(j, q):
                if not isinstance(j, int) or j >= 0:
                    par, u = q // B, q % B
                    done = j * SLOTS + (q + 1)
                    act.wait_ge(pre, done)
                    nc.scalar.activation(gate[:], gsum2[par][:].rearrange("p (c e) -> p c e", c=KC)[:, :, u * NG * S:(u + 1) * NG * S],
                                         ACT.Tanh, scale=UNSCALE).then_inc(gates, 1)
                if isinstance(j, int):
                    prepare(SLOTS * j + K_SCAN + q)
                for k, stage in stages:
                    at = group_of(j, q, k)
                    if at is not None:
                        stage(j, *at)

            run_slots(act, slot)

            act.wait_ge(y_done, 1)
            nc.scalar.activation(y32[:], bankA[:, 0:D], ACT.Copy, scale=UNSCALE).then_inc(y_ready, 1)
            act.wait_ge(y_ready, 1)
            nc.scalar.activation(yhl[:, 0], y32[:], ACT.Copy).then_inc(y_hi, 1)
            for g in range(G):
                act.wait_ge(o2_done, g + 1)
                at_least(act, r2_ready, g - 3)
                nc.scalar.activation(t32[:, g % 4], tail_banks[g % 4][:, 0:D], ACT.Tanh, scale=UNSCALE).then_inc(t_ready, 1)

        @block.tensor
        def _(pe):
            PAIR = ((0, 0), (0, 1), (1, 0))

            def mm(o, lhsT, rhs, start):
                return nc.tensor.matmul(o, lhsT, rhs, start=start, stop=False, skip_group_check=True)

            wt = {n: whl[n][:].rearrange("p a (k e) -> p a k e", k=PC if n == "tok" else KC) for n in w_shapes}
            w_parts = {n: len(scaled(n)) for n in w_shapes}

            def weights(n):
                pe.wait_ge(w_lo[n], w_parts[n])

            def filling(T):
                if T == K_XHI_A:
                    pe.wait_ge(small_in, 16 * 8)
                    nc.tensor.matmul(bankB[0:TAPS, 0:H], coef_sb[:], wpos_sb[:], start=True, stop=True).then_inc(pos_m1, 1)
                    pe.wait_ge(pos_m1x, 1)
                    for c in range(KC):
                        last = nc.tensor.matmul(bankB[:, c * S:(c + 1) * S], m1[:, c * HC:(c + 1) * HC, :], proto_sb[:],
                                                start=True, stop=True)
                    last.then_inc(pos_e, 1)
                    pe.wait_ge(pos_ex, 1)
                    weights("tok")
                    pe.wait_ge(b_row, 16)
                    pe.wait_ge(b_hi, len(bias_parts))
                    pe.wait_ge(const_set, 1)
                    pe.wait_ge(eye_set, 2)
                for k, n in ((min(QK_MM), "qkv"), (min(WO_MM), "out"), (min(XP), "gx"), (K_SCAN - 1, "gu")):
                    if T == k:
                        weights(n)

            def embed(lo, hi):
                def stage(j, g, p):
                    if lo == 0:
                        at_least(pe, h0_ready, g)
                    pe.wait_ge(x_split, g * 2 + (1 if hi <= PC // 2 else 2))
                    for c in range(lo, hi):
                        for a, b in PAIR:
                            last = mm(emb_ps, xhl[:, a, c], wt["tok"][:, b, c], c == 0 and a == 0 and b == 0)
                    if hi == PC:
                        mm(emb_ps, ones2[:], bias2[:, 0:D], False).then_inc(emb_done, 1)
                return stage

            def transpose_h0(j, g, p):
                pe.wait_ge(h0_split, g + 1)
                bank_free(pe, g, K_TH0, bankC_use)
                for a in range(2):
                    for c in range(KC):
                        last = nc.tensor.transpose(th_ps[:, 0, a, c], h0hl[:, a, c * P:(c + 1) * P], eye16[:])
                last.then_inc(th0_done, 1)

            def queries_keys(lo, hi):
                def stage(j, g, p):
                    if lo == 0:
                        pe.wait_ge(h0T_ready, g + 1)
                        bank_free(pe, g, min(QK_MM), bankD_use)
                    for m in range(lo, hi):
                        for k in range(KC):
                            for a, b in PAIR:
                                last = mm(bankD[:, m * TOK:(m + 1) * TOK], wt["qkv"][:, a, k, m * P:(m + 1) * P],
                                          h0T[:, b, k], k == 0 and a == 0 and b == 0)
                    if hi == 2 * KC:
                        last.then_inc(qk_done, 1)
                return stage

            def values(lo, hi):
                def stage(j, g, p):
                    if lo == 0:
                        pe.wait_ge(h0T_ready, g + 1)
                        bank_free(pe, g, min(V_MM), bankC_use)
                    for k in range(lo, hi):
                        for a, b in PAIR:
                            last = mm(v_ps, h0T[:, a, k], wt["qkv"][:, b, k, 2 * D:], k == 0 and a == 0 and b == 0)
                    if hi == KC:
                        last.then_inc(v_done, 1)
                return stage

            def scores(lo, hi):
                def stage(j, g, p):
                    if lo == 0:
                        for done, runs in ((qx_ready, QX), (qx_act, QX_ACT)):
                            if runs:
                                pe.wait_ge(done, (g + 1) * len(runs))
                        bank_free(pe, g, min(S_MM), bankB_use)
                    for n in range(lo, hi):
                        c, b = divmod(n, B)
                        for x, y in PAIR:
                            last = mm(s_ps[:, c * TOK + b * S:c * TOK + (b + 1) * S], qx[:, x, c, b::B],
                                      kT[:, y, c, b * S:(b + 1) * S], x == 0 and y == 0)
                    if hi == KC * B:
                        last.then_inc(s_done, 1)
                return stage

            def transpose_p(j, g, p):
                pe.wait_ge(e_split, g + 1)
                bank_free(pe, g, K_TP, bankC_use)
                for a in range(2):
                    for c in range(KC):
                        last = nc.tensor.transpose(th_ps[:, 0, a, c], ehl[:, a, c * TOK:(c + 1) * TOK], eye16[:])
                last.then_inc(tp_done, 1)

            def attend(lo, hi):
                def stage(j, g, p):
                    if lo == 0:
                        for done, runs in ((px_ready, PX), (px_act, PX_ACT)):
                            if runs:
                                pe.wait_ge(done, (g + 1) * len(runs))
                        pe.wait_ge(v_ready, g + 1)
                        bank_free(pe, g, min(PV_MM), bankD_use)
                    for n in range(lo, hi):
                        c, h = divmod(n, HC)
                        for x, y in PAIR:
                            last = mm(pv_ps[:, n], px[:, x, c, h::HC], v[:, p, y, n], x == 0 and y == 0)
                    if hi == H:
                        last.then_inc(pv_done, 1)
                return stage

            def transpose_o(j, g, p):
                pe.wait_ge(o_split, g + 1)
                bank_free(pe, g, K_TO, bankB_use)
                for a in range(2):
                    for c in range(KC):
                        last = nc.tensor.transpose(to_ps[:, a, c], ohl[:, a, c * P:(c + 1) * P], eye16[:])
                last.then_inc(to_done, 1)

            def project_out(lo, hi):
                def stage(j, g, p):
                    if lo == 0:
                        pe.wait_ge(oT_ready, g + 1)
                        bank_free(pe, g, min(WO_MM), bankB_use)
                    for k in range(lo, hi):
                        for a, b in PAIR:
                            last = mm(wo_ps, oT[:, a, k], wt["out"][:, b, k], k == 0 and a == 0 and b == 0)
                    if hi == KC:
                        last.then_inc(wo_done, 1)
                return stage

            def transpose_h1(j, g, p):
                pe.wait_ge(h1_split, g + 1)
                bank_free(pe, g, K_TH1, bankC_use)
                for a in range(2):
                    for c in range(KC):
                        last = nc.tensor.transpose(th_ps[:, 1, a, c], h1hl[:, a, c * P:(c + 1) * P], eye16[:])
                last.then_inc(th1_done, 1)

            h1v = h1T[:].rearrange("p (a c t) -> p a c t", a=2, c=KC)

            def gate_inputs(lo, hi):
                def stage(j, g, p):
                    if lo == 0:
                        pe.wait_ge(h1T_ready, g + 1)
                    for n in range(lo, hi):
                        c, m = divmod(n, NG)
                        o = gsum[p][c][:, 0:B * NG * S].rearrange("p (u m s) -> p u m s", u=B, m=NG)[:, :, m]
                        mm(o, bias2[:, D + n * P:D + (n + 1) * P], ones2[:], m == 0)
                        for k in range(KC):
                            for a, b in PAIR:
                                last = mm(o, wt["gx"][:, a, k, n * P:(n + 1) * P], h1v[:, b, k], False)
                    if hi == KC * NG:
                        last.then_inc(xp_done, 1)
                return stage

            stages = tuple((k, stage) for table in ((XP, gate_inputs), (K_TH1, transpose_h1), (WO_MM, project_out),
                                                    (K_TO, transpose_o), (PV_MM, attend), (K_TP, transpose_p),
                                                    (S_MM, scores), (V_MM, values), (QK_MM, queries_keys),
                                                    (K_TH0, transpose_h0), (EMB, embed))
                           for k, stage in ([(k, table[1](*run)) for k, run in table[0].items()]
                                            if isinstance(table[0], dict) else [table]))

            def scan_step(j, q):
                par, u = q // B, q % B
                t = j * SLOTS + q

                def add(c, k, low):
                    for m in range(NG):
                        o = gsum[par][c][:, (u * NG + m) * S:(u * NG + m + 1) * S]
                        cols = slice((c * NG + m) * P, (c * NG + m + 1) * P)
                        if low:
                            last = mm(o, wt["gu"][:, 0, k, cols], slo[:, k], False)
                        else:
                            mm(o, wt["gu"][:, 0, k, cols], shi[:, k], False)
                            last = mm(o, wt["gu"][:, 1, k, cols], shi[:, k], False)
                    return last

                pe.wait_ge(s_hi, t + 1)
                for c in range(KC):
                    for k in range(KC):
                        add(c, k, False)
                pe.wait_ge(s_lo, t + 1)
                for c in range(KC):
                    for k in range(KC):
                        last = add(c, k, True)
                last.then_inc(pre, 1)

            def slot(j, q):
                if not isinstance(j, int) or j >= 0:
                    scan_step(j, q)
                if isinstance(j, int):
                    filling(SLOTS * j + K_SCAN + q)
                for k, stage in stages:
                    at = group_of(j, q, k)
                    if at is not None:
                        stage(j, *at)

            run_slots(pe, slot)

            weights("ou")
            pe.wait_ge(cx_ready, 2)
            for k in range(KC):
                for a, b in PAIR:
                    mm(bankA[:, 0:D], cx[:, a, k], wt["ou"][:, b, k], k == 0 and a == 0 and b == 0)
            mm(bankA[:, 0:D], ones2[:], bias2[:, D + NG * D:], False).then_inc(y_done, 1)
            weights("ox")
            pe.wait_ge(h1T_kept, 16 * G)
            hk = h1Tall[:].rearrange("p (g a c t) -> p g a c t", g=G, a=2, c=KC)
            pe.wait_ge(gates, G * B)
            for g in range(G):
                o = tail_banks[g % 4][:, 0:D]
                at_least(pe, t_ready, g - 3)
                for k in range(KC):
                    for a, b in PAIR:
                        mm(o, hk[:, g, a, k], wt["ox"][:, b, k], k == 0 and a == 0 and b == 0)
                if g == 0:
                    pe.wait_ge(y_split, 1)
                mm(o, eyew[:], yhl[:, 0], False)
                mm(o, eyew[:], yhl[:, 1], False).then_inc(o2_done, 1)

        @block.vector
        def _(dve):
            def weight_lo(n):
                for i, (part, scale) in enumerate(scaled(n)):
                    dve.wait_ge(w_hi[n], i + 1)
                    nc.vector.scalar_tensor_tensor(part(whl[n][:, 1]), part(w32[n][:]), scale, part(whl[n][:, 0]),
                                                   ALU.mult, ALU.subtract).then_inc(w_lo[n], 1)

            def prepare(T):
                if T == K_XHI_A:
                    nc.vector.memset(ones2[:], 1.0).then_inc(const_set, 1)
                    nc.vector.memset(minus_half[:], -0.5).then_inc(const_set, 1)
                    nc.vector.memset(eps[:], EPS).then_inc(const_set, 1)
                    nc.vector.memset(v[:, :, 0], 1.0).then_inc(const_set, 1)
                    nc.vector.memset(v[:, :, 1], 0.0).then_inc(const_set, 1)
                    dve.wait_ge(pos_m1, 1)
                    nc.vector.tensor_copy(m1[:], bankB[0:TAPS, 0:H].unsqueeze(2).broadcast_to([TAPS, H, S])).then_inc(pos_m1x, 1)
                    for i, (lo, hi, scale) in enumerate(bias_parts):
                        dve.wait_ge(b_hi, i + 1)
                        nc.vector.scalar_tensor_tensor(brow_lo[:, lo:hi], brow32[:, lo:hi], scale, bias2[0:1, lo:hi],
                                                       ALU.mult, ALU.subtract).then_inc(b_lo, 1)
                    dve.wait_ge(pos_e, 1)
                    nc.vector.tensor_copy(ed[:].rearrange("p c d -> p (c d)"), bankB[:, 0:KC * S]).then_inc(pos_ex, 1)
                    dve.wait_ge(pos_ex, 1)
                    for c in range(KC):
                        bc = inc_sb[:, c:c + 1].broadcast_to([P, S])
                        last_hi = nc.vector.tensor_scalar(shi[:, c], bc, 2.0, None, ALU.mult)
                        last_32 = nc.vector.tensor_scalar(s32[:, c], bc, 2.0, None, ALU.mult)
                    last_hi.then_inc(s_hi, 1)
                    last_32.then_inc(s_32, 1)
                    dve.wait_ge(s_32, 1)
                    nc.vector.tensor_tensor(slo[:], s32[:], shi[:], ALU.subtract).then_inc(s_lo, 1)
                if T == 1:
                    for c in range(KC):
                        at_least(dve, pos_set, c)
                        nc.vector.tensor_tensor(picked[:], pick_sb[:], ed[:, c].unsqueeze(1).broadcast_to([P, S, S]),
                                                ALU.mult).then_inc(pos_pick, 1)
                        dve.wait_ge(pos_pick, c + 1)
                        nc.vector.reduce_sum(posb[:, c], picked[:], AX_X).then_inc(pos_set, 1)
                for k, n in ((K_XHI_A, "tok"), (3, "qkv"), (14, "out"), (20, "gx"), (22, "gu"), (24, "ox"), (25, "ou")):
                    if T == k:
                        weight_lo(n)

            def qk_pair_lo(j, g, p):
                dve.wait_ge(qk_hi, g + 1)
                for c in range(KC):
                    nc.vector.scalar_tensor_tensor(qT[:, 1, c].rearrange("p s b -> p b s"),
                                                   q_ps[:, c * TOK:(c + 1) * TOK].rearrange("p (b s) -> p b s", b=B),
                                                   UNSCALE, qT[:, 0, c].rearrange("p s b -> p b s"),
                                                   ALU.mult, ALU.subtract)
                nc.vector.scalar_tensor_tensor(kT[:, 1].rearrange("p c t -> p (c t)"), k_ps, UNSCALE,
                                               kT[:, 0].rearrange("p c t -> p (c t)"),
                                               ALU.mult, ALU.subtract).then_inc(qk_lo, 1)

            def spread_q(run):
                def stage(j, g, p):
                    q_wait(dve, g)
                    for h in range(*run):
                        last = nc.vector.tensor_scalar(qx[:, :, :, h * TOK:(h + 1) * TOK], q_flat,
                                                       block_sb[:, h:h + 1], None, ALU.mult)
                    last.then_inc(qx_ready, 1)
                return stage

            def spread_p(run):
                def stage(j, g, p):
                    p_wait(dve, g)
                    for b in range(*run):
                        last = nc.vector.tensor_scalar(px[:, :, :, b * P:(b + 1) * P], p_flat,
                                                       block_sb[:, b:b + 1], None, ALU.mult)
                    last.then_inc(px_ready, 1)
                return stage

            def v_pair_lo(j, g, p):
                dve.wait_ge(v_hi, g + 1)
                nc.vector.scalar_tensor_tensor(v[:, p, 1, :, 0:HD], v_ps.rearrange("p (h w) -> p h w", w=HD), UNSCALE,
                                               v[:, p, 0, :, 0:HD], ALU.mult, ALU.subtract).then_inc(v_ready, 1)

            def softmax_shift(j, g, p):
                dve.wait_ge(s_done, g + 1)
                if isinstance(g, int) and g == 0:
                    dve.wait_ge(pos_set, KC)
                for c in range(KC):
                    last = nc.vector.tensor_tensor(sc[:, c], s_ps.rearrange("p (c b j) -> p c b j", c=KC, b=B)[:, c],
                                                   posb[:, c].unsqueeze(1).broadcast_to([P, B, S]), ALU.add)
                last.then_inc(sc_ready, 1)
                dve.wait_ge(sc_ready, g + 1)
                nc.vector.reduce_max(mx[:], sc[:], AX_X).then_inc(mx_ready, 1)
                dve.wait_ge(mx_ready, g + 1)
                at_least(dve, e_ready, g)
                nc.vector.tensor_tensor(scm[:], sc[:], mx[:].unsqueeze(3).broadcast_to([P, KC, B, S]),
                                        ALU.subtract).then_inc(scm_ready, 1)

            def divide_sum(j, g, p):
                dve.wait_ge(pv_done, g + 1)
                nc.vector.reciprocal(rs[:], pv_ps[:, :, HD]).then_inc(rs_ready, 1)
                dve.wait_ge(rs_ready, g + 1)
                at_least(dve, o_split, g)
                nc.vector.tensor_tensor(o32[:].rearrange("p (h w) -> p h w", w=HD), pv_ps[:, :, 0:HD],
                                        rs[:].unsqueeze(2).broadcast_to([P, H, HD]), ALU.mult).then_inc(o_ready, 1)

            def residual_stats(j, g, p):
                h = hall[:, bass.ds(g * D, D)]
                dve.wait_ge(wo_done, g + 1)
                nc.vector.scalar_tensor_tensor(r1[:], wo_ps, UNSCALE, h, ALU.mult, ALU.add).then_inc(r1_ready, 1)
                dve.wait_ge(r1_ready, g + 1)
                nc.vector.bn_stats(stats[:], r1[:]).then_inc(st1_ready, 1)
                dve.wait_ge(st1_ready, g + 1)
                dve.sem_inc(st1_seen, 1)
                nc.vector.bn_aggr(mv[:], stats[:]).then_inc(mv1_ready, 1)

            def first_norm(j, g, p):
                h = hall[:, bass.ds(g * D, D)]
                dve.wait_ge(rstd1_ready, g + 1)
                nc.vector.tensor_scalar(h, r1[:], mv[:, 0:1], rstd[:], ALU.subtract, ALU.mult).then_inc(h1_ready, 1)

            stages = ((K_H1, first_norm), (K_LN, residual_stats), (K_O, divide_sum), (K_SM, softmax_shift),
                      (K_VOUT, v_pair_lo),
                      (K_QK, qk_pair_lo), *((k, spread_p(run)) for k, run in PX.items()),
                      *((k, spread_q(run)) for k, run in QX.items()))

            def scan_state(j, q):
                t = j * SLOTS + (q + 1)

                dve.wait_ge(gates, t)
                nc.vector.scalar_tensor_tensor(keepf[:], gate[:, :, 0:S], 1.0, s32[:], ALU.add, ALU.mult)
                nc.vector.scalar_tensor_tensor(inp[:], gate[:, :, S:2 * S], 1.0, gate[:, :, 2 * S:3 * S],
                                               ALU.add, ALU.mult).then_inc(addends, 1)
                dve.wait_ge(addends, t)
                nc.vector.scalar_tensor_tensor(shi[:], keepf[:], 0.5, inp[:], ALU.mult, ALU.add).then_inc(s_hi, 1)
                nc.vector.scalar_tensor_tensor(s32[:], keepf[:], 0.5, inp[:], ALU.mult, ALU.add).then_inc(s_32, 1)
                dve.wait_ge(s_32, t + 1)
                nc.vector.tensor_tensor(slo[:], s32[:], shi[:], ALU.subtract).then_inc(s_lo, 1)

            def slot(j, q):
                if not isinstance(j, int) or j >= 0:
                    scan_state(j, q)
                if isinstance(j, int):
                    prepare(SLOTS * j + K_SCAN + q)
                for k, stage in stages:
                    at = group_of(j, q, k)
                    if at is not None:
                        stage(j, *at)

            run_slots(dve, slot)

            n = G * B + 1
            dve.wait_ge(s_lo, n)
            for a, s_ in ((0, shi), (1, slo)):
                nc.vector.tensor_copy(cx[:, a], s_[:].unsqueeze(2).broadcast_to([P, KC, B, S])).then_inc(cx_ready, 1)

            def finish(g):
                i = g % 4
                dve.wait_ge(rstd2_ready, g + 1)
                if g >= 4:
                    dve.wait_ge(out_in[i], 16 * (g // 4))
                nc.vector.tensor_scalar(res[:, i], r2[:, i], mv2[:, i, 0:1], rstd2[:, i:i + 1], ALU.subtract,
                                        ALU.mult).then_inc(res_ready, 1)

            for g in range(G):
                i = g % 4
                dve.wait_ge(t_ready, g + 1)
                nc.vector.tensor_tensor(r2[:, i], t32[:, i], hall[:, g * D:(g + 1) * D], ALU.add).then_inc(r2_ready, 1)
                dve.wait_ge(r2_ready, g + 1)
                nc.vector.bn_stats(stats2[:, i], r2[:, i]).then_inc(st2_ready, 1)
                dve.wait_ge(st2_ready, g + 1)
                nc.vector.bn_aggr(mv2[:, i], stats2[:, i]).then_inc(mv2_ready, 1)
                if g >= 2:
                    finish(g - 2)
            finish(G - 2)
            finish(G - 1)

        @block.gpsimd
        def _(pool):
            def x_pair_lo(half):
                def stage(j, g, p):
                    pool.wait_ge(x_hi, g * 2 + (half + 1))
                    c = slice(half * PC // 2, (half + 1) * PC // 2)
                    nc.gpsimd.tensor_tensor(xhl[:, 1, c], x32[:, p, c], xhl[:, 0, c], ALU.subtract).then_inc(x_split, 1)
                return stage

            def h0_pair_lo(j, g, p):
                pool.wait_ge(h0_ready, g + 1)
                nc.gpsimd.tensor_tensor(h0hl[:, 1], hall[:, bass.ds(g * D, D)], h0hl[:, 0], ALU.subtract).then_inc(h0_split, 1)

            def e_pair_lo(j, g, p):
                pool.wait_ge(e_hi, g + 1)
                nc.gpsimd.tensor_tensor(ehl[:, 1], e32[:], ehl[:, 0], ALU.subtract).then_inc(e_split, 1)

            def o_pair_lo(j, g, p):
                pool.wait_ge(o_hi, g + 1)
                nc.gpsimd.tensor_tensor(ohl[:, 1], o32[:], ohl[:, 0], ALU.subtract).then_inc(o_split, 1)

            def rstd1(j, g, p):
                pool.wait_ge(mv1_ready, g + 1)
                nc.gpsimd.tensor_tensor(veps[:], mv[:, 1:2], eps[:], ALU.add).then_inc(ve1_ready, 1)
                pool.wait_ge(ve1_ready, g + 1)
                nc.gpsimd.tensor_tensor(rstd[:], veps[:], minus_half[:], ALU.pow).then_inc(rstd1_ready, 1)

            def h1_pair_lo(j, g, p):
                pool.wait_ge(h1_hi, g + 1)
                nc.gpsimd.tensor_tensor(h1hl[:, 1], hall[:, bass.ds(g * D, D)], h1hl[:, 0], ALU.subtract).then_inc(h1_split, 1)

            pool.wait_ge(const_set, 3)

            stages = ((K_H1HL, h1_pair_lo), (K_LN, rstd1), (K_OHL, o_pair_lo), (K_EXP, e_pair_lo), (K_H0, h0_pair_lo),
                      (K_XHI_A, x_pair_lo(0)), (K_XHI_B, x_pair_lo(1)))

            def slot(j, q):
                for k, stage in stages:
                    at = group_of(j, q, k)
                    if at is not None:
                        stage(j, *at)

            run_slots(pool, slot)

            pool.wait_ge(y_hi, 1)
            nc.gpsimd.tensor_tensor(yhl[:, 1], y32[:], yhl[:, 0], ALU.subtract).then_inc(y_split, 1)
            for g in range(G):
                i = g % 4
                pool.wait_ge(mv2_ready, g + 1)
                nc.gpsimd.tensor_scalar(veps2[:, i:i + 1], mv2[:, i, 1:2], EPS, None, ALU.add).then_inc(ve2_ready, 1)
                pool.wait_ge(ve2_ready, g + 1)
                nc.gpsimd.tensor_tensor(rstd2[:, i:i + 1], veps2[:, i:i + 1], minus_half[:], ALU.pow).then_inc(rstd2_ready, 1)


def kernel(x, L0_tok_W, L0_tok_b, L0_attn_Wqkv, L0_attn_Wout, L0_attn_Wpos, L0_attn_coeffs,
           L0_ffn_wf, L0_ffn_uf, L0_ffn_bf, L0_ffn_wi, L0_ffn_ui, L0_ffn_bi, L0_ffn_wc, L0_ffn_uc, L0_ffn_bc,
           L0_ffn_wo, L0_ffn_uo, L0_ffn_bo, L0_ffn_in_c):
    import numpy as np
    import concourse.bacc as bacc
    from concourse.bass_utils import run_bass_kernel_spmd

    def rows(w, chunks):
        w = np.asarray(w)
        return np.ascontiguousarray(w.T.reshape(chunks, P, w.shape[0]).transpose(1, 0, 2).reshape(P, -1))

    def gates_of(ws):
        w = np.stack([np.asarray(a) for a in ws])
        w = w.reshape(NG, KC, P, KC, P).transpose(4, 3, 1, 0, 2)
        return np.ascontiguousarray(w.reshape(P, -1))

    x = np.asarray(x)
    blocks = x.reshape(x.shape[0], 3, 4, 16, 4, 16).transpose(0, 1, 2, 4, 3, 5)
    patches = blocks.reshape(G, TOK, PC, P)
    xT = np.ascontiguousarray(patches.transpose(3, 0, 2, 1).reshape(P, -1))
    gb = np.stack([np.asarray(a) for a in (L0_ffn_bf, L0_ffn_bi, L0_ffn_bc)]).reshape(NG, KC, P).transpose(1, 0, 2)
    brow = np.concatenate([np.asarray(L0_tok_b), gb.reshape(-1), np.asarray(L0_ffn_bo)]).reshape(1, -1)

    idx = np.clip(np.round(np.arange(S, dtype=np.float32) / np.float32(S - 1) * (RES - 1)).astype(int), 0, RES - 1)
    ramp = np.linspace(0.0, 1.0, RES).astype(np.float32)
    lag = idx[None, :] - np.arange(TAPS)[:, None]
    protoT = np.where(lag >= 0, ramp[np.maximum(lag, 0)], 0).astype(np.float32)
    i, jj, d = np.meshgrid(np.arange(S), np.arange(S), np.arange(S), indexing="ij")
    pick = np.tile((np.abs(i - jj) == d).astype(np.float32).reshape(S, S * S), (HC, 1))

    blocks16 = np.repeat(np.eye(HC, dtype=np.float32), HD, axis=0)

    arrays = {
        "xT": xT, "w_tok": rows(L0_tok_W, PC), "w_qkv": rows(L0_attn_Wqkv, KC), "w_out": rows(L0_attn_Wout, KC),
        "w_gx": gates_of((L0_ffn_wf, L0_ffn_wi, L0_ffn_wc)), "w_gu": gates_of((L0_ffn_uf, L0_ffn_ui, L0_ffn_uc)),
        "w_ox": rows(L0_ffn_wo, KC), "w_ou": rows(L0_ffn_uo, KC), "brow": brow,
        "in_c": np.ascontiguousarray(np.asarray(L0_ffn_in_c).reshape(KC, P).T),
        "coeffs": np.asarray(L0_attn_coeffs), "wpos": np.ascontiguousarray(np.asarray(L0_attn_Wpos).T),
        "protoT": protoT, "pick": pick, "blocks": blocks16, "eye": np.eye(P, dtype=np.float32),
    }
    nc = bacc.Bacc("TRN2", target_bir_lowering=False, num_devices=1)
    args = {n: nc.dram_tensor(n + "_dram", a.shape, mybir.dt.from_np(a.dtype), kind="ExternalInput").ap()
            for n, a in arrays.items()}
    out = nc.dram_tensor("out_dram", (G * TOK, D), F32, kind="ExternalOutput").ap()
    vit_layer(nc, **args, out=out)
    r = run_bass_kernel_spmd(nc, [{n + "_dram": a for n, a in arrays.items()}], core_ids=[0])
    return r.results[0]["out_dram"].reshape(x.shape[0], S, D)
```

```python
from contextlib import ExitStack

import concourse.bass as bass
from concourse import mybir
from concourse.alu_op_type import AluOpType as ALU

ACT = mybir.ActivationFunctionType
F32 = mybir.dt.float32
F16 = mybir.dt.float16
AX_X = mybir.AxisListType.X

P = 128
D = 256
KC = D // P
S = 16
B = 8
TOK = B * S
G = 16
H = 16
HD = D // H
HC = H // KC
PC = 6
NG = 3
TAPS, RES, NF = 101, 128, 4
VW = HD + 1

WSCALE = 256.0
UNSCALE = 1.0 / WSCALE
EPS = 1e-5

WARM = {-3: 10, -1: 3, 0: 3, 1: 3, 2: 3, 3: 3, 4: 3, 6: 3, 7: 3, 19: 1, 31: 1}
XO_AT = (27, 22, 14, 12, 20, 18, 11, 9, 3, 2, 1, 0)
OX_AT, OU_AT = 29, 5
K_XHI_A = -3
K_XHI_B = -2
EMB = {-2: (0, 1), -1: (1, 3), 0: (3, 4), 1: (4, 5), 4: (5, 6)}
K_H0 = 4
K_TH0 = 7
K_H0T = 7
QK_MM = {8: (0, 2), 9: (2, 4)}
K_QK = 10
QX = {11: (0, 4), 12: (4, 6)}
QX_ACT = {12: (6, 8)}
V_MM = {12: (0, 2)}
K_VOUT = 13
S_MM = {13: (0, 11), 14: (11, 16)}
K_SM = 15
K_EXP = 16
K_TP = 17
K_PT = 17
PX = {17: (0, 3), 18: (3, 5)}
PX_ACT = {18: (5, 7), 19: (7, 8)}
PV_MM = {20: (0, 8), 21: (8, 12), 22: (12, 16)}
K_O = 22
K_OHL = 23
K_TO = 24
K_OT = 25
WO_MM = {26: (0, 2)}
K_LN = 27
K_H1 = 28
K_H1HL = 29
K_TH1 = 30
K_H1T = 30
XP = {31: (0, 1), 34: (1, 2), 35: (2, 6)}
K_SCAN = 36
K_PQKV = 3
K_PGX = 8
K_POUT = 7
K_PGU = 6
K_POS = 4
K_PBIAS = -1
SLOTS = 2 * B
PAIRS = G // 2
LAST = K_SCAN + G * B - 1
XO = {LAST - before_end: g for g, before_end in enumerate(XO_AT)}
W_PREP = ((K_XHI_A, "tokA"), (K_XHI_A + 1, "tokB"), (K_PQKV, "qkv"), (K_PGX, "gx"), (K_POUT, "out"), (K_PGU, "gu"),
          (LAST - OX_AT, "ox"), (LAST - OU_AT, "ou"))
TAIL_LAG = 4


def staged(*tables):
    return [(k, make(*run) if run else make) for slots, make in tables
            for k, run in (slots.items() if isinstance(slots, dict) else ((slots, None),))]


def at_least(eng, sem, value):
    if isinstance(value, int) and value <= 0:
        return
    eng.wait_ge(sem, value)


def upto(value):
    return min(value, G) if isinstance(value, int) else value


def run_slots(eng, slot):
    first = -((K_SCAN - K_XHI_A + SLOTS - 1) // SLOTS)
    full = PAIRS - (K_SCAN + SLOTS - 1 - K_XHI_A) // SLOTS
    for j in range(first, 0):
        for q in range(SLOTS):
            slot(j, q)
    with eng.Fori(0, full) as j:
        for q in range(SLOTS):
            slot(j, q)
    for j in range(full, PAIRS):
        for q in range(SLOTS):
            slot(j, q)


def before(k, other):
    return (k - other - 1) // B + 1


def bank_free(eng, g, k, holders):
    for slot, read in holders:
        at_least(eng, read, upto(g + before(k, slot)))


def group_of(j, q, k):
    d, r = divmod(K_SCAN + q - k, B)
    if r:
        return None
    if isinstance(j, int):
        g = 2 * j + d
        return (g, d % 2) if 0 <= g < G else None
    return (j * 2 + d, d % 2)


def vit_layer(nc, xT, w_tok, w_qkv, w_out, w_gx, w_gu, w_ox, w_ou, brow, in_c, coeffs, wpos,
              protoT, pick, blocks, eye, out):
    with ExitStack() as ctx:
        def sb(name, shape, dt):
            return ctx.enter_context(nc.sbuf_tensor(name, shape, dt))

        def bank(name):
            return ctx.enter_context(nc.psum_tensor(name, [P, 512], F32))

        def sem(name):
            return ctx.enter_context(nc.semaphore(name))

        w_shapes = {"tokA": PC // 2 * D, "tokB": PC // 2 * D, "qkv": KC * 3 * D, "out": KC * D, "gx": KC * NG * D,
                    "gu": KC * NG * D, "ox": KC * D, "ou": KC * D}
        w_dram = {"tokA": w_tok[:, 0:PC // 2 * D], "tokB": w_tok[:, PC // 2 * D:],
                  "qkv": w_qkv, "out": w_out, "gx": w_gx, "gu": w_gu, "ox": w_ox, "ou": w_ou}
        w32 = {n: sb("w32_" + n, [P, c], F32) for n, c in w_shapes.items()}
        whl = {n: sb("whl_" + n, [P, 2, c], F16) for n, c in w_shapes.items()}
        NB = D + NG * D + D
        brow32 = sb("brow32", [2, NB], F32)
        bhi = sb("bhi", [2, NB], F16)
        bias2 = sb("bias2", [2, NB], F16)
        zeros = sb("zeros", [P, 512], F16)
        minus2 = sb("minus2", [2, P], F16)

        eye32 = sb("eye32", [P, P], F32)
        eye16 = sb("eye16", [P, P], F16)
        eyew = sb("eyew", [P, P], F16)
        coef_sb = sb("coef_sb", [NF, TAPS], F32)
        wpos_sb = sb("wpos_sb", [NF, H], F32)
        proto_sb = sb("proto_sb", [TAPS, S], F32)
        pick_sb = sb("pick_sb", [P, S, S], F32)
        m1 = sb("m1", [TAPS, H, S], F32)
        ed = sb("ed", [P, KC, S], F32)
        picked = sb("picked", [P, S, S], F32)
        posb = sb("posb", [P, KC, S], F32)
        block_sb = sb("block_sb", [P, HC], F32)
        minus_half = sb("minus_half", [P, 1], F32)
        eps = sb("eps", [P, 1], F32)

        x32 = sb("x32", [P, 2, PC, TOK], F32)
        xhl = sb("xhl", [P, 2, PC, TOK], F16)
        hall = sb("hall", [P, G * D], F32)
        h0hl = sb("h0hl", [P, 2, D], F16)
        h0T = sb("h0T", [P, 2, KC, TOK], F16)
        qT = sb("qT", [P, 2, KC, S, B], F16)
        kT = sb("kT", [P, 2, KC, TOK], F16)
        v = sb("v", [P, 2, 2, H, VW], F16)
        qx = sb("qx", [P, 2, KC, HC * S * B], F16)
        sc = sb("sc", [P, KC, B, S], F32)
        mx = sb("mx", [P, KC, B], F32)
        scm = sb("scm", [P, KC, B, S], F32)
        e32 = sb("e32", [P, KC * TOK], F32)
        ehl = sb("ehl", [P, 2, KC * TOK], F16)
        pT = sb("pT", [P, 2, KC, S, HC], F16)
        px = sb("px", [P, 2, KC, B * S * HC], F16)
        rs = sb("rs", [P, H], F32)
        o32 = sb("o32", [P, D], F32)
        ohl = sb("ohl", [P, 2, D], F16)
        oT = sb("oT", [P, 2, KC, TOK], F16)
        r1 = sb("r1", [P, D], F32)
        stats = sb("stats", [P, 6], F32)
        mv = sb("mv", [P, 2], F32)
        veps = sb("veps", [P, 1], F32)
        rstd = sb("rstd", [P, 1], F32)
        h1hl = sb("h1hl", [P, 2, D], F16)
        h1T = sb("h1T", [P, 2 * KC * TOK], F16)
        h1Tall = sb("h1Tall", [P, G * 2 * KC * TOK], F16)

        inc_sb = sb("inc_sb", [P, KC], F32)
        s32 = sb("s32", [P, KC, S], F32)
        shi = sb("shi", [P, KC, S], F16)
        slo = sb("slo", [P, KC, S], F16)
        gate = sb("gate", [P, KC, NG * S], F32)
        keepf = sb("keepf", [P, KC, S], F32)
        inp = sb("inp", [P, KC, S], F32)

        cx = sb("cx", [P, 2, KC, B, S], F16)
        yhl = sb("yhl", [P, 2, D], F16)
        t32 = sb("t32", [P, G, D], F32)
        stats2 = sb("stats2", [P, G, 6], F32)
        mv2 = sb("mv2", [P, G, 2], F32)
        veps2 = sb("veps2", [P, G], F32)
        rstd2 = sb("rstd2", [P, G], F32)
        shift2 = sb("shift2", [P, G], F32)

        gsum2 = [ctx.enter_context(nc.psum_tensor(f"gsum{p}", [P, KC * 512], F32)) for p in range(2)]
        gsum = [[t[:, c * 512:(c + 1) * 512] for c in range(KC)] for t in gsum2]
        bankA, bankB, bankC, bankD = bank("bankA"), bank("bankB"), bank("bankC"), bank("bankD")
        y_ps = gsum[1][1][:, 0:D]
        pair_banks = [bankA[:], bankB[:], bankD[:], bankC[:]] + gsum[0] + gsum[1]
        emb_ps = bankA[:, 0:D]
        s_ps = bankB[:, 0:KC * TOK]
        to_ps = bankB[:].bitcast(F16)[:, 0:512].rearrange("p (a c t) -> p a c t", a=2, c=KC)
        wo_ps = bankB[:, 0:D]
        th_ps = bankC[:].bitcast(F16).rearrange("p (w a c t) -> p w a c t", w=2, a=2, c=KC)
        v_ps = bankC[:, 0:D]
        q_ps, k_ps = bankD[:, 0:KC * TOK], bankD[:, KC * TOK:]
        pv_ps = bankD[:, 0:H * VW].rearrange("p (h w) -> p h w", w=VW)

        w_in = {n: sem("w_in_" + n) for n in w_shapes}
        b_in, eye_in, small_in = sem("b_in"), sem("eye_in"), sem("small_in")
        w_hi = {n: sem("w_hi_" + n) for n in w_shapes}
        w_lo = {n: sem("w_lo_" + n) for n in w_shapes}
        zeros_set = sem("zeros_set")
        const_set, eye_set = sem("const_set"), sem("eye_set")
        b_hi, b_set = sem("b_hi"), sem("b_set")
        pos_m1, pos_m1x, pos_e, pos_ex, pos_pick, pos_set = (
            sem("pos_m1"), sem("pos_m1x"), sem("pos_e"), sem("pos_ex"), sem("pos_pick"), sem("pos_set"))
        x_in = [sem("x_in0"), sem("x_in1")]
        x_hi, x_split = sem("x_hi"), sem("x_split")
        emb_done, h0_ready, h0_split = sem("emb_done"), sem("h0_ready"), sem("h0_split")
        th0_done, h0T_ready = sem("th0_done"), sem("h0T_ready")
        qk_done, qk_hi, qk_lo, qx_ready = sem("qk_done"), sem("qk_hi"), sem("qk_lo"), sem("qx_ready")
        v_done, v_hi, v_ready = sem("v_done"), sem("v_hi"), sem("v_ready")
        s_done, sc_ready, mx_ready, scm_ready = sem("s_done"), sem("sc_ready"), sem("mx_ready"), sem("scm_ready")
        e_ready, e_hi, e_split = sem("e_ready"), sem("e_hi"), sem("e_split")
        tp_done, pT_ready, px_ready = sem("tp_done"), sem("pT_ready"), sem("px_ready")
        pv_done, rs_ready, o_ready, o_hi, o_split = (
            sem("pv_done"), sem("rs_ready"), sem("o_ready"), sem("o_hi"), sem("o_split"))
        to_done, oT_ready = sem("to_done"), sem("oT_ready")
        wo_done, r1_ready, st1_ready, st1_seen, mv1_ready, ve1_ready, rstd1_ready = (
            sem("wo_done"), sem("r1_ready"), sem("st1_ready"), sem("st1_seen"), sem("mv1_ready"), sem("ve1_ready"),
            sem("rstd1_ready"))
        h1_ready, h1_hi, h1_split = sem("h1_ready"), sem("h1_hi"), sem("h1_split")
        th1_done, h1T_ready, h1T_kept, xp_done = (
            sem("th1_done"), sem("h1T_ready"), sem("h1T_kept"), sem("xp_done"))
        pre, gates, addends = sem("pre"), sem("gates"), sem("addends")
        s_hi, s_32, s_lo = sem("s_hi"), sem("s_32"), sem("s_lo")
        cx_ready, y_done, y_hi, y_split = sem("cx_ready"), sem("y_done"), sem("y_hi"), sem("y_split")
        o2_done, t_ready, r2_ready, st2_ready, mv2_ready, ve2_ready, rstd2_ready, shift2_ready, res_ready = (
            sem("o2_done"), sem("t_ready"), sem("r2_ready"), sem("st2_ready"), sem("mv2_ready"),
            sem("ve2_ready"), sem("rstd2_ready"), sem("shift2_ready"), sem("res_ready"))
        out_in = sem("out_in")

        qx_act, px_act = sem("qx_act"), sem("px_act")
        bankB_use = ((min(S_MM), sc_ready), (K_TO, oT_ready), (min(WO_MM), r1_ready))
        bankC_use = ((K_TH0, h0T_ready), (min(V_MM), v_ready), (K_TP, pT_ready), (K_TH1, h1T_ready))
        bankD_use = ((min(QK_MM), qk_lo), (min(PV_MM), o_ready))
        q_flat = qT[:].rearrange("p a c s b -> p a c (s b)")
        p_flat = pT[:].rearrange("p a c s h -> p a c (s h)")

        def q_wait(eng, g):
            eng.wait_ge(qk_lo, g + 1)

        def p_wait(eng, g):
            eng.wait_ge(pT_ready, g + 1)

        block = ctx.enter_context(nc.Block())

        def scaled(n):
            if n == "qkv":
                w = lambda t: t.rearrange("p (k e) -> p k e", k=KC)
                return [(lambda t: w(t)[:, :, 0:D], WSCALE * HD ** -0.5), (lambda t: w(t)[:, :, D:3 * D], WSCALE)]
            if n in ("gx", "gu"):
                f = 1.0 if n == "gx" else 0.5
                w = lambda t: t.rearrange("p (k e) -> p k e", e=NG * P)
                return [(lambda t: w(t)[:, :, 0:2 * P], WSCALE * 0.5 * f), (lambda t: w(t)[:, :, 2 * P:], WSCALE * f)]
            return [(lambda t: t, WSCALE * (0.5 if n == "ou" else 1.0))]

        def gate_bias(t):
            return t[:, D:D + NG * D].rearrange("a (c e) -> a c e", c=KC)

        bias_cols = (slice(0, D), slice(D, NB))
        bias_parts = [[(lambda t: t[:, 0:D], WSCALE)],
                      [(lambda t: gate_bias(t)[:, :, 0:2 * P], WSCALE * 0.5),
                      (lambda t: gate_bias(t)[:, :, 2 * P:], WSCALE), (lambda t: t[:, D + NG * D:], WSCALE)]]

        def bias_count(i):
            return sum(len(parts) + 1 for parts in bias_parts[:i + 1])

        @block.sync
        def _(sp):
            xg = xT.rearrange("p (g c) -> p g c", g=G)
            sp.dma_start(w32["tokA"][:], w_dram["tokA"]).then_inc(w_in["tokA"], 16)
            sp.dma_start(x32[:, 0].rearrange("p c t -> p (c t)"), xg[:, 0, :]).then_inc(x_in[0], 16)
            sp.dma_start(w32["tokB"][:], w_dram["tokB"]).then_inc(w_in["tokB"], 16)
            sp.dma_start(eye32[:], eye).then_inc(eye_in, 16)
            sp.dma_start(brow32[:], brow).then_inc(b_in, 16)
            sp.dma_start(w32["qkv"][:], w_qkv).then_inc(w_in["qkv"], 16)
            sp.dma_start(x32[:, 1].rearrange("p c t -> p (c t)"), xg[:, 1, :]).then_inc(x_in[1], 16)
            for t, a in ((coef_sb, coeffs), (wpos_sb, wpos), (proto_sb, protoT), (inc_sb, in_c), (block_sb, blocks)):
                sp.dma_start(t[:], a).then_inc(small_in, 16)
            sp.dma_start(pick_sb[:].rearrange("p j d -> p (j d)"), pick).then_inc(small_in, 16)
            for n in ("gx", "out", "gu", "ox", "ou"):
                sp.dma_start(w32[n][:], w_dram[n]).then_inc(w_in[n], 16)

            def load_x(j, g, p):
                at_least(sp, x_split, g * 2 - 2)
                sp.dma_start(x32[:, p].rearrange("p c t -> p (c t)"),
                             xT[:, bass.ds(g * (PC * TOK), PC * TOK)]).then_inc(x_in[p], 16)

            def keep_h1T(j, g, p):
                sp.wait_ge(h1T_ready, g + 1)
                w = 2 * KC * TOK
                sp.dma_start(h1Tall[:, bass.ds(g * w, w)], h1T[:]).then_inc(h1T_kept, 16)

            def slot(j, q):
                for k, stage in ((K_H1T, keep_h1T), (-B, load_x)):
                    at = group_of(j, q, k)
                    if at is None or (stage is load_x and isinstance(at[0], int) and at[0] < 2):
                        continue
                    stage(j, *at)

            run_slots(sp, slot)

            for n in range(PAIRS):
                sp.wait_ge(res_ready, n + 1)
                sp.dma_start(out[2 * n * TOK:2 * (n + 1) * TOK, :].rearrange("(w t) d -> t w d", w=2),
                             t32[:, 2 * n:2 * n + 2]).then_inc(out_in, 16)
            sp.wait_ge(out_in, 16 * PAIRS)

        @block.scalar
        def _(act):
            def weight_hi(n):
                act.wait_ge(w_in[n], 16)
                for part, scale in scaled(n):
                    nc.scalar.activation(part(whl[n][:, 0]), part(w32[n][:]), ACT.Copy, scale=scale).then_inc(w_hi[n], 1)

            def prepare(T):
                for k, n in W_PREP:
                    if T == k:
                        weight_hi(n)
                if T == K_PBIAS:
                    act.wait_ge(eye_in, 16)
                    nc.scalar.activation(eye16[:], eye32[:], ACT.Copy).then_inc(eye_set, 1)
                    nc.scalar.activation(eyew[:], eye32[:], ACT.Copy, scale=WSCALE).then_inc(eye_set, 1)
                    act.wait_ge(b_in, 16)
                    bias_hi(0)
                if T == K_PBIAS + 1:
                    bias_hi(1)

            def bias_hi(i):
                for part, scale in bias_parts[i]:
                    nc.scalar.activation(part(brow32), part(brow32), ACT.Copy, scale=scale).then_inc(b_hi, 1)
                act.wait_ge(b_hi, bias_count(i) - 1)
                nc.scalar.activation(bhi[:, bias_cols[i]], brow32[:, bias_cols[i]], ACT.Copy).then_inc(b_hi, 1)

            def x_pair_hi(half):
                def stage(j, g, p):
                    if half == 0:
                        act.wait_ge(x_in[p], g * 8 + (16 - 8 * p))
                    at_least(act, emb_done, g)
                    c = slice(half * PC // 2, (half + 1) * PC // 2)
                    nc.scalar.activation(xhl[:, 0, c], x32[:, p, c], ACT.Copy).then_inc(x_hi, 1)
                return stage

            def h0_out(j, g, p):
                act.wait_ge(emb_done, g + 1)
                at_least(act, th0_done, g)
                nc.scalar.activation(hall[:, bass.ds(g * D, D)], emb_ps, ACT.Copy, scale=UNSCALE)
                nc.scalar.activation(h0hl[:, 0], emb_ps, ACT.Copy, scale=UNSCALE).then_inc(h0_ready, 1)

            def h0T_out(j, g, p):
                act.wait_ge(th0_done, g + 1)
                at_least(act, v_done, g)
                nc.scalar.activation(h0T[:], th_ps[:, 0], ACT.Copy).then_inc(h0T_ready, 1)

            def qk_out(j, g, p):
                act.wait_ge(qk_done, g + 1)
                at_least(act, s_done, g)
                nc.scalar.activation(kT[:, 0], k_ps.rearrange("p (c t) -> p c t", c=KC), ACT.Copy, scale=UNSCALE)
                nc.scalar.activation(qT[:, 0].rearrange("p c s b -> p c b s"),
                                     q_ps.rearrange("p (c b s) -> p c b s", c=KC, b=B), ACT.Copy,
                                     scale=UNSCALE).then_inc(qk_hi, 1)

            def spread(dst, src, waits, done):
                def run_stage(lo, hi):
                    def stage(j, g, p):
                        waits(act, g)
                        for h in range(lo, hi):
                            last = nc.scalar.activation(dst[:, :, :, h * P:(h + 1) * P], src, ACT.Copy,
                                                        scale=block_sb[:, h:h + 1])
                        last.then_inc(done, 1)
                    return stage
                return run_stage

            def v_out(j, g, p):
                act.wait_ge(v_done, g + 1)
                at_least(act, pv_done, g - 1)
                nc.scalar.activation(v[:, p, 0, :, 0:HD], v_ps.rearrange("p (h w) -> p h w", w=HD), ACT.Copy,
                                     scale=UNSCALE).then_inc(v_hi, 1)

            def exponential(j, g, p):
                act.wait_ge(scm_ready, g + 1)
                at_least(act, e_split, g)
                nc.scalar.activation(e32[:], scm[:].rearrange("p c b j -> p (c b j)"), ACT.Exp).then_inc(e_ready, 1)
                act.wait_ge(e_ready, g + 1)
                at_least(act, tp_done, g)
                nc.scalar.activation(ehl[:, 0], e32[:], ACT.Copy).then_inc(e_hi, 1)

            def pT_out(j, g, p):
                act.wait_ge(tp_done, g + 1)
                at_least(act, pv_done, g)
                nc.scalar.activation(pT[:].rearrange("p a c s h -> p (a c) h s"),
                                     th_ps[:, 0].rearrange("p a c (h s) -> p (a c) h s", h=HC),
                                     ACT.Copy).then_inc(pT_ready, 1)

            def o_pair_hi(j, g, p):
                act.wait_ge(o_ready, g + 1)
                at_least(act, to_done, g)
                nc.scalar.activation(ohl[:, 0], o32[:], ACT.Copy).then_inc(o_hi, 1)

            def oT_out(j, g, p):
                act.wait_ge(to_done, g + 1)
                at_least(act, wo_done, g)
                nc.scalar.activation(oT[:], to_ps, ACT.Copy).then_inc(oT_ready, 1)

            def h1_pair_hi(j, g, p):
                act.wait_ge(h1_ready, g + 1)
                at_least(act, th1_done, g)
                nc.scalar.activation(h1hl[:, 0], hall[:, bass.ds(g * D, D)], ACT.Copy).then_inc(h1_hi, 1)

            def h1T_out(j, g, p):
                act.wait_ge(th1_done, g + 1)
                at_least(act, xp_done, g)
                at_least(act, h1T_kept, g * 16)
                nc.scalar.activation(h1T[:], th_ps[:, 1].rearrange("p a c t -> p (a c t)"), ACT.Copy).then_inc(h1T_ready, 1)

            stages = staged(
                (K_H1T, h1T_out),
                (K_H1HL, h1_pair_hi),
                (K_OT, oT_out),
                (K_OHL, o_pair_hi),
                (K_EXP, exponential),
                (QX_ACT, spread(qx, q_flat, q_wait, qx_act)),
                (K_QK, qk_out),
                (PX_ACT, spread(px, p_flat, p_wait, px_act)),
                (K_H0T, h0T_out),
                (K_VOUT, v_out),
                (K_PT, pT_out),
                (K_H0, h0_out),
                (K_XHI_A, x_pair_hi(0)),
                (K_XHI_B, x_pair_hi(1)),
            )

            def slot(j, q):
                if not isinstance(j, int) or j >= 0:
                    par, u = q // B, q % B
                    done = j * SLOTS + (q + 1)
                    act.wait_ge(pre, done)
                    sums = gsum2[par][:].rearrange("p (c e) -> p c e", c=KC)
                    nc.scalar.activation(gate[:], sums[:, :, u * NG * S:(u + 1) * NG * S],
                                         ACT.Tanh, scale=UNSCALE).then_inc(gates, 1)
                if isinstance(j, int):
                    prepare(SLOTS * j + K_SCAN + q)
                for k, stage in stages:
                    at = group_of(j, q, k)
                    if at is not None:
                        stage(j, *at)

            run_slots(act, slot)

            act.wait_ge(y_done, 1)
            nc.scalar.activation(yhl[:, 0], y_ps, ACT.Copy, scale=UNSCALE).then_inc(y_hi, 1)

            def norm(n):
                act.wait_ge(shift2_ready, n + 1)
                for g in (2 * n, 2 * n + 1):
                    last = nc.scalar.activation(t32[:, g], t32[:, g], ACT.Identity, scale=rstd2[:, g:g + 1],
                                                bias=shift2[:, g:g + 1])
                last.then_inc(res_ready, 1)

            for n in range(PAIRS):
                act.wait_ge(o2_done, n + 1)
                nc.scalar.activation(t32[:, 2 * n:2 * n + 2], pair_banks[n].rearrange("p (w d) -> p w d", w=2), ACT.Tanh,
                                     scale=UNSCALE).then_inc(t_ready, 1)
                if n >= TAIL_LAG:
                    norm(n - TAIL_LAG)
            for n in range(PAIRS - TAIL_LAG, PAIRS):
                norm(n)

        @block.tensor
        def _(pe):
            PAIR = ((0, 0), (0, 1), (1, 0))

            def mm(o, lhsT, rhs, start):
                return nc.tensor.matmul(o, lhsT, rhs, start=start, stop=False, skip_group_check=True)

            wt = {n: whl[n][:].rearrange("p a (k e) -> p a k e", k=PC // 2 if n.startswith("tok") else KC) for n in w_shapes}
            w_parts = {n: len(scaled(n)) for n in w_shapes}

            def weights(n):
                pe.wait_ge(w_lo[n], w_parts[n])

            def filling(T):
                if T == K_XHI_A:
                    pe.wait_ge(zeros_set, 1)
                for _ in range(WARM.get(T, 0)):
                    mm(gsum[1][1], zeros[:, 0:P], zeros[:], True)
                if T == min(EMB):
                    weights("tokA")
                if T == min(k for k, run in EMB.items() if run[1] > PC // 2):
                    weights("tokB")
                if T == max(EMB):
                    pe.wait_ge(b_set, 1)
                if T == K_TH0:
                    pe.wait_ge(eye_set, 2)
                if T == min(XP):
                    pe.wait_ge(b_set, 2)
                if T == K_POS:
                    pe.wait_ge(small_in, 16 * 6)
                    nc.tensor.matmul(bankB[0:TAPS, 0:H], coef_sb[:], wpos_sb[:], start=True, stop=True).then_inc(pos_m1, 1)
                if T == K_POS + 1:
                    pe.wait_ge(pos_m1x, 1)
                    for c in range(KC):
                        last = nc.tensor.matmul(bankB[:, c * S:(c + 1) * S], m1[:, c * HC:(c + 1) * HC, :], proto_sb[:],
                                                start=True, stop=True)
                    last.then_inc(pos_e, 1)
                if T == min(S_MM):
                    pe.wait_ge(pos_ex, 1)
                for k, n in ((min(QK_MM), "qkv"), (min(WO_MM), "out"), (min(XP), "gx"), (K_SCAN - 1, "gu")):
                    if T == k:
                        weights(n)
                if T in XO:
                    g = XO[T]
                    if g == 0:
                        weights("ox")
                    pe.wait_ge(h1T_kept, 16 * (g + 1))
                    if g % 2 == 0:
                        for read in pair_free[g // 2]:
                            pe.wait_ge(read, G)
                    outputs_x(XO[T])

            pair_free = [(h0_ready,), *([read for _, read in use] for use in (bankB_use, bankD_use, bankC_use)), (), ()]
            hk = h1Tall[:].rearrange("p (g a c t) -> p g a c t", g=G, a=2, c=KC)

            def outputs_x(g):
                o = pair_banks[g // 2][:, (g % 2) * D:(g % 2 + 1) * D]
                for k in range(KC):
                    for a, b in PAIR:
                        mm(o, hk[:, g, a, k], wt["ox"][:, b, k], g % 2 == 0 and k == 0 and a == 0 and b == 0)

            def embed(lo, hi):
                def stage(j, g, p):
                    if lo == 0:
                        at_least(pe, h0_ready, g)
                    pe.wait_ge(x_split, g * 2 + (1 if hi <= PC // 2 else 2))
                    for c in range(lo, hi):
                        for a, b in PAIR:
                            last = mm(emb_ps, xhl[:, a, c], wt[("tokA", "tokB")[c // (PC // 2)]][:, b, c % (PC // 2)], c == 0 and a == 0 and b == 0)
                    if hi == PC:
                        mm(emb_ps, minus2[:], bias2[:, 0:D], False).then_inc(emb_done, 1)
                return stage

            def transpose_h0(j, g, p):
                pe.wait_ge(h0_split, g + 1)
                bank_free(pe, g, K_TH0, bankC_use)
                for a in range(2):
                    for c in range(KC):
                        last = nc.tensor.transpose(th_ps[:, 0, a, c], h0hl[:, a, c * P:(c + 1) * P], eye16[:])
                last.then_inc(th0_done, 1)

            def queries_keys(lo, hi):
                def stage(j, g, p):
                    if lo == 0:
                        pe.wait_ge(h0T_ready, g + 1)
                        bank_free(pe, g, min(QK_MM), bankD_use)
                    for m in range(lo, hi):
                        for k in range(KC):
                            for a, b in PAIR:
                                last = mm(bankD[:, m * TOK:(m + 1) * TOK], wt["qkv"][:, a, k, m * P:(m + 1) * P],
                                          h0T[:, b, k], k == 0 and a == 0 and b == 0)
                    if hi == 2 * KC:
                        last.then_inc(qk_done, 1)
                return stage

            def values(lo, hi):
                def stage(j, g, p):
                    if lo == 0:
                        pe.wait_ge(h0T_ready, g + 1)
                        bank_free(pe, g, min(V_MM), bankC_use)
                    for k in range(lo, hi):
                        for a, b in PAIR:
                            last = mm(v_ps, h0T[:, a, k], wt["qkv"][:, b, k, 2 * D:], k == 0 and a == 0 and b == 0)
                    if hi == KC:
                        last.then_inc(v_done, 1)
                return stage

            def scores(lo, hi):
                def stage(j, g, p):
                    if lo == 0:
                        for done, runs in ((qx_ready, QX), (qx_act, QX_ACT)):
                            if runs:
                                pe.wait_ge(done, (g + 1) * len(runs))
                        bank_free(pe, g, min(S_MM), bankB_use)
                    for n in range(lo, hi):
                        c, b = divmod(n, B)
                        for x, y in PAIR:
                            last = mm(s_ps[:, c * TOK + b * S:c * TOK + (b + 1) * S], qx[:, x, c, b::B],
                                      kT[:, y, c, b * S:(b + 1) * S], x == 0 and y == 0)
                    if hi == KC * B:
                        last.then_inc(s_done, 1)
                return stage

            def transpose_p(j, g, p):
                pe.wait_ge(e_split, g + 1)
                bank_free(pe, g, K_TP, bankC_use)
                for a in range(2):
                    for c in range(KC):
                        last = nc.tensor.transpose(th_ps[:, 0, a, c], ehl[:, a, c * TOK:(c + 1) * TOK], eye16[:])
                last.then_inc(tp_done, 1)

            def attend(lo, hi):
                def stage(j, g, p):
                    if lo == 0:
                        for done, runs in ((px_ready, PX), (px_act, PX_ACT)):
                            if runs:
                                pe.wait_ge(done, (g + 1) * len(runs))
                        pe.wait_ge(v_ready, g + 1)
                        bank_free(pe, g, min(PV_MM), bankD_use)
                    for n in range(lo, hi):
                        c, h = divmod(n, HC)
                        for x, y in PAIR:
                            last = mm(pv_ps[:, n], px[:, x, c, h::HC], v[:, p, y, n], x == 0 and y == 0)
                    if hi == H:
                        last.then_inc(pv_done, 1)
                return stage

            def transpose_o(j, g, p):
                pe.wait_ge(o_split, g + 1)
                bank_free(pe, g, K_TO, bankB_use)
                for a in range(2):
                    for c in range(KC):
                        last = nc.tensor.transpose(to_ps[:, a, c], ohl[:, a, c * P:(c + 1) * P], eye16[:])
                last.then_inc(to_done, 1)

            def project_out(lo, hi):
                def stage(j, g, p):
                    if lo == 0:
                        pe.wait_ge(oT_ready, g + 1)
                        bank_free(pe, g, min(WO_MM), bankB_use)
                    for k in range(lo, hi):
                        for a, b in PAIR:
                            last = mm(wo_ps, oT[:, a, k], wt["out"][:, b, k], k == 0 and a == 0 and b == 0)
                    if hi == KC:
                        last.then_inc(wo_done, 1)
                return stage

            def transpose_h1(j, g, p):
                pe.wait_ge(h1_split, g + 1)
                bank_free(pe, g, K_TH1, bankC_use)
                for a in range(2):
                    for c in range(KC):
                        last = nc.tensor.transpose(th_ps[:, 1, a, c], h1hl[:, a, c * P:(c + 1) * P], eye16[:])
                last.then_inc(th1_done, 1)

            h1v = h1T[:].rearrange("p (a c t) -> p a c t", a=2, c=KC)

            def gate_inputs(lo, hi):
                def stage(j, g, p):
                    if lo == 0:
                        pe.wait_ge(h1T_ready, g + 1)
                    for n in range(lo, hi):
                        c, m = divmod(n, NG)
                        o = gsum[p][c][:, 0:B * NG * S].rearrange("p (u m s) -> p u m s", u=B, m=NG)[:, :, m]
                        mm(o, bias2[:, D + n * P:D + (n + 1) * P], minus2[:], m == 0)
                        for k in range(KC):
                            for a, b in PAIR:
                                last = mm(o, wt["gx"][:, a, k, n * P:(n + 1) * P], h1v[:, b, k], False)
                    if hi == KC * NG:
                        last.then_inc(xp_done, 1)
                return stage

            stages = staged(
                (XP, gate_inputs),
                (K_TH1, transpose_h1),
                (WO_MM, project_out),
                (PV_MM, attend),
                (K_TP, transpose_p),
                (S_MM, scores),
                (K_TH0, transpose_h0),
                (QK_MM, queries_keys),
                (V_MM, values),
                (K_TO, transpose_o),
                (EMB, embed),
            )

            def scan_step(j, q):
                par, u = q // B, q % B
                t = j * SLOTS + q

                def add(c, k, low):
                    for m in range(NG):
                        o = gsum[par][c][:, (u * NG + m) * S:(u * NG + m + 1) * S]
                        cols = slice((c * NG + m) * P, (c * NG + m + 1) * P)
                        if low:
                            last = mm(o, wt["gu"][:, 0, k, cols], slo[:, k], False)
                        else:
                            mm(o, wt["gu"][:, 0, k, cols], shi[:, k], False)
                            last = mm(o, wt["gu"][:, 1, k, cols], shi[:, k], False)
                    return last

                pe.wait_ge(s_hi, t + 1)
                for c in range(KC):
                    for k in range(KC):
                        add(c, k, False)
                pe.wait_ge(s_lo, t + 1)
                for c in range(KC):
                    for k in range(KC):
                        last = add(c, k, True)
                last.then_inc(pre, 1)

            def slot(j, q):
                if not isinstance(j, int) or j >= 0:
                    scan_step(j, q)
                if isinstance(j, int):
                    filling(SLOTS * j + K_SCAN + q)
                for k, stage in stages:
                    at = group_of(j, q, k)
                    if at is not None:
                        stage(j, *at)

            run_slots(pe, slot)

            weights("ou")
            pe.wait_ge(gates, G * B)
            pe.wait_ge(cx_ready, 2)
            for k in range(KC):
                for a, b in PAIR:
                    mm(y_ps, cx[:, a, k], wt["ou"][:, b, k], k == 0 and a == 0 and b == 0)
            mm(y_ps, minus2[:], bias2[:, D + NG * D:], False).then_inc(y_done, 1)
            pe.wait_ge(h1T_kept, 16 * G)
            outputs_x(G - 4)
            outputs_x(G - 3)
            pe.wait_ge(y_split, 1)
            for n in range(PAIRS):
                if n == PAIRS - 1:
                    outputs_x(G - 2)
                    outputs_x(G - 1)
                for a in range(2):
                    last = mm(pair_banks[n], eyew[:], yhl[:, a].unsqueeze(1).broadcast_to([P, 2, D]), False)
                last.then_inc(o2_done, 1)

        @block.vector
        def _(dve):
            def weight_lo(n):
                for i, (part, scale) in enumerate(scaled(n)):
                    dve.wait_ge(w_hi[n], i + 1)
                    nc.vector.scalar_tensor_tensor(part(whl[n][:, 1]), part(w32[n][:]), scale, part(whl[n][:, 0]),
                                                   ALU.mult, ALU.subtract).then_inc(w_lo[n], 1)

            def bias_pair(i):
                dve.wait_ge(b_hi, bias_count(i))
                c = bias_cols[i]
                nc.vector.scalar_tensor_tensor(bias2[:, c], bhi[:, c], eye32[0:2, 1:2], brow32[:, c], ALU.mult,
                                               ALU.subtract).then_inc(b_set, 1)

            def prepare(T):
                if T == K_XHI_A:
                    nc.vector.memset(zeros[:], 0.0).then_inc(zeros_set, 1)
                    nc.vector.memset(minus2[:], -1.0).then_inc(const_set, 1)
                    nc.vector.memset(minus_half[:], -0.5).then_inc(const_set, 1)
                    nc.vector.memset(eps[:], EPS).then_inc(const_set, 1)
                if T == K_PBIAS:
                    dve.wait_ge(eye_in, 16)
                    bias_pair(0)
                if T == K_PBIAS + 1:
                    bias_pair(1)
                    nc.vector.memset(v[:, :, 0], 1.0).then_inc(const_set, 1)
                    nc.vector.memset(v[:, :, 1], 0.0).then_inc(const_set, 1)
                if T == K_POS:
                    dve.wait_ge(pos_m1, 1)
                    nc.vector.tensor_copy(m1[:], bankB[0:TAPS, 0:H].unsqueeze(2).broadcast_to([TAPS, H, S])).then_inc(pos_m1x, 1)
                if T == K_POS + 1:
                    dve.wait_ge(pos_e, 1)
                    nc.vector.tensor_copy(ed[:].rearrange("p c d -> p (c d)"), bankB[:, 0:KC * S]).then_inc(pos_ex, 1)
                    dve.wait_ge(pos_ex, 1)
                    for c in range(KC):
                        bc = inc_sb[:, c:c + 1].broadcast_to([P, S])
                        last_hi = nc.vector.tensor_scalar(shi[:, c], bc, 2.0, None, ALU.mult)
                        last_32 = nc.vector.tensor_scalar(s32[:, c], bc, 2.0, None, ALU.mult)
                    last_hi.then_inc(s_hi, 1)
                    last_32.then_inc(s_32, 1)
                    dve.wait_ge(s_32, 1)
                    nc.vector.tensor_tensor(slo[:], s32[:], shi[:], ALU.subtract).then_inc(s_lo, 1)
                if T == K_POS + 2:
                    for c in range(KC):
                        at_least(dve, pos_set, c)
                        nc.vector.tensor_tensor(picked[:], pick_sb[:], ed[:, c].unsqueeze(1).broadcast_to([P, S, S]),
                                                ALU.mult).then_inc(pos_pick, 1)
                        dve.wait_ge(pos_pick, c + 1)
                        nc.vector.reduce_sum(posb[:, c], picked[:], AX_X).then_inc(pos_set, 1)
                for k, n in W_PREP:
                    if T == k:
                        weight_lo(n)

            def qk_pair_lo(j, g, p):
                dve.wait_ge(qk_hi, g + 1)
                for c in range(KC):
                    nc.vector.scalar_tensor_tensor(qT[:, 1, c].rearrange("p s b -> p b s"),
                                                   q_ps[:, c * TOK:(c + 1) * TOK].rearrange("p (b s) -> p b s", b=B),
                                                   UNSCALE, qT[:, 0, c].rearrange("p s b -> p b s"),
                                                   ALU.mult, ALU.subtract)
                nc.vector.scalar_tensor_tensor(kT[:, 1].rearrange("p c t -> p (c t)"), k_ps, UNSCALE,
                                               kT[:, 0].rearrange("p c t -> p (c t)"),
                                               ALU.mult, ALU.subtract).then_inc(qk_lo, 1)

            def spread_q(lo, hi):
                def stage(j, g, p):
                    q_wait(dve, g)
                    for h in range(lo, hi):
                        last = nc.vector.tensor_scalar(qx[:, :, :, h * TOK:(h + 1) * TOK], q_flat,
                                                       block_sb[:, h:h + 1], None, ALU.mult)
                    last.then_inc(qx_ready, 1)
                return stage

            def spread_p(lo, hi):
                def stage(j, g, p):
                    p_wait(dve, g)
                    for b in range(lo, hi):
                        last = nc.vector.tensor_scalar(px[:, :, :, b * P:(b + 1) * P], p_flat,
                                                       block_sb[:, b:b + 1], None, ALU.mult)
                    last.then_inc(px_ready, 1)
                return stage

            def v_pair_lo(j, g, p):
                dve.wait_ge(v_hi, g + 1)
                nc.vector.scalar_tensor_tensor(v[:, p, 1, :, 0:HD], v_ps.rearrange("p (h w) -> p h w", w=HD), UNSCALE,
                                               v[:, p, 0, :, 0:HD], ALU.mult, ALU.subtract).then_inc(v_ready, 1)

            def softmax_shift(j, g, p):
                dve.wait_ge(s_done, g + 1)
                if isinstance(g, int) and g == 0:
                    dve.wait_ge(pos_set, KC)
                for c in range(KC):
                    last = nc.vector.tensor_tensor(sc[:, c], s_ps.rearrange("p (c b j) -> p c b j", c=KC, b=B)[:, c],
                                                   posb[:, c].unsqueeze(1).broadcast_to([P, B, S]), ALU.add)
                last.then_inc(sc_ready, 1)
                dve.wait_ge(sc_ready, g + 1)
                nc.vector.reduce_max(mx[:], sc[:], AX_X).then_inc(mx_ready, 1)
                dve.wait_ge(mx_ready, g + 1)
                at_least(dve, e_ready, g)
                nc.vector.tensor_tensor(scm[:], sc[:], mx[:].unsqueeze(3).broadcast_to([P, KC, B, S]),
                                        ALU.subtract).then_inc(scm_ready, 1)

            def divide_sum(j, g, p):
                dve.wait_ge(pv_done, g + 1)
                nc.vector.reciprocal(rs[:], pv_ps[:, :, HD]).then_inc(rs_ready, 1)
                dve.wait_ge(rs_ready, g + 1)
                at_least(dve, o_split, g)
                nc.vector.tensor_tensor(o32[:].rearrange("p (h w) -> p h w", w=HD), pv_ps[:, :, 0:HD],
                                        rs[:].unsqueeze(2).broadcast_to([P, H, HD]), ALU.mult).then_inc(o_ready, 1)

            def residual_stats(j, g, p):
                h = hall[:, bass.ds(g * D, D)]
                dve.wait_ge(wo_done, g + 1)
                nc.vector.scalar_tensor_tensor(r1[:], wo_ps, UNSCALE, h, ALU.mult, ALU.add).then_inc(r1_ready, 1)
                dve.wait_ge(r1_ready, g + 1)
                nc.vector.bn_stats(stats[:], r1[:]).then_inc(st1_ready, 1)
                dve.wait_ge(st1_ready, g + 1)
                dve.sem_inc(st1_seen, 1)
                nc.vector.bn_aggr(mv[:], stats[:]).then_inc(mv1_ready, 1)

            def first_norm(j, g, p):
                h = hall[:, bass.ds(g * D, D)]
                dve.wait_ge(rstd1_ready, g + 1)
                nc.vector.tensor_scalar(h, r1[:], mv[:, 0:1], rstd[:], ALU.subtract, ALU.mult).then_inc(h1_ready, 1)

            stages = staged(
                (K_O, divide_sum),
                (K_LN, residual_stats),
                (K_SM, softmax_shift),
                (K_VOUT, v_pair_lo),
                (K_QK, qk_pair_lo),
                (PX, spread_p),
                (QX, spread_q),
                (K_H1, first_norm),
            )

            def scan_state(j, q):
                t = j * SLOTS + (q + 1)

                dve.wait_ge(gates, t)
                nc.vector.scalar_tensor_tensor(keepf[:], gate[:, :, 0:S], 1.0, s32[:], ALU.add, ALU.mult)
                nc.vector.scalar_tensor_tensor(inp[:], gate[:, :, S:2 * S], 1.0, gate[:, :, 2 * S:3 * S],
                                               ALU.add, ALU.mult).then_inc(addends, 1)
                dve.wait_ge(addends, t)
                nc.vector.scalar_tensor_tensor(shi[:], keepf[:], 0.5, inp[:], ALU.mult, ALU.add).then_inc(s_hi, 1)
                nc.vector.scalar_tensor_tensor(s32[:], keepf[:], 0.5, inp[:], ALU.mult, ALU.add).then_inc(s_32, 1)
                dve.wait_ge(s_32, t + 1)
                nc.vector.tensor_tensor(slo[:], s32[:], shi[:], ALU.subtract).then_inc(s_lo, 1)

            def slot(j, q):
                if not isinstance(j, int) or j >= 0:
                    scan_state(j, q)
                if isinstance(j, int):
                    prepare(SLOTS * j + K_SCAN + q)
                for k, stage in stages:
                    at = group_of(j, q, k)
                    if at is not None:
                        stage(j, *at)

            run_slots(dve, slot)

            n = G * B + 1
            dve.wait_ge(s_lo, n)
            for a, s_ in ((0, shi), (1, slo)):
                nc.vector.tensor_copy(cx[:, a], s_[:].unsqueeze(2).broadcast_to([P, KC, B, S])).then_inc(cx_ready, 1)

            dve.wait_ge(y_hi, 1)
            nc.vector.scalar_tensor_tensor(yhl[:, 1], y_ps, UNSCALE, yhl[:, 0], ALU.mult, ALU.subtract).then_inc(y_split, 1)
            hg = hall[:].rearrange("p (g d) -> p g d", g=G)

            def stats_of(n):
                dve.wait_ge(r2_ready, n + 1)
                for g in (2 * n, 2 * n + 1):
                    nc.vector.bn_stats(stats2[:, g], t32[:, g]).then_inc(st2_ready, 1)

            def moments(n):
                for g in (2 * n, 2 * n + 1):
                    dve.wait_ge(st2_ready, g + 1)
                    nc.vector.bn_aggr(mv2[:, g], stats2[:, g]).then_inc(mv2_ready, 1)

            def shift(n):
                dve.wait_ge(rstd2_ready, n + 1)
                w = slice(2 * n, 2 * n + 2)
                nc.vector.scalar_tensor_tensor(shift2[:, w], mv2[:, w, 0], -1.0, rstd2[:, w], ALU.mult,
                                               ALU.mult).then_inc(shift2_ready, 1)

            for n in range(PAIRS + 2):
                if n < PAIRS:
                    dve.wait_ge(t_ready, n + 1)
                    w = slice(2 * n, 2 * n + 2)
                    nc.vector.tensor_tensor(t32[:, w], t32[:, w], hg[:, w], ALU.add).then_inc(r2_ready, 1)
                if 1 <= n <= PAIRS:
                    stats_of(n - 1)
                    moments(n - 1)
                if n >= 2:
                    shift(n - 2)

        @block.gpsimd
        def _(pool):
            def x_pair_lo(half):
                def stage(j, g, p):
                    pool.wait_ge(x_hi, g * 2 + (half + 1))
                    c = slice(half * PC // 2, (half + 1) * PC // 2)
                    nc.gpsimd.tensor_tensor(xhl[:, 1, c], x32[:, p, c], xhl[:, 0, c], ALU.subtract).then_inc(x_split, 1)
                return stage

            def h0_pair_lo(j, g, p):
                pool.wait_ge(h0_ready, g + 1)
                nc.gpsimd.tensor_tensor(h0hl[:, 1], hall[:, bass.ds(g * D, D)], h0hl[:, 0], ALU.subtract).then_inc(h0_split, 1)

            def e_pair_lo(j, g, p):
                pool.wait_ge(e_hi, g + 1)
                nc.gpsimd.tensor_tensor(ehl[:, 1], e32[:], ehl[:, 0], ALU.subtract).then_inc(e_split, 1)

            def o_pair_lo(j, g, p):
                pool.wait_ge(o_hi, g + 1)
                nc.gpsimd.tensor_tensor(ohl[:, 1], o32[:], ohl[:, 0], ALU.subtract).then_inc(o_split, 1)

            def rstd1(j, g, p):
                pool.wait_ge(mv1_ready, g + 1)
                nc.gpsimd.tensor_tensor(veps[:], mv[:, 1:2], eps[:], ALU.add).then_inc(ve1_ready, 1)
                pool.wait_ge(ve1_ready, g + 1)
                nc.gpsimd.tensor_tensor(rstd[:], veps[:], minus_half[:], ALU.pow).then_inc(rstd1_ready, 1)

            def h1_pair_lo(j, g, p):
                pool.wait_ge(h1_hi, g + 1)
                nc.gpsimd.tensor_tensor(h1hl[:, 1], hall[:, bass.ds(g * D, D)], h1hl[:, 0], ALU.subtract).then_inc(h1_split, 1)

            pool.wait_ge(const_set, 3)

            stages = staged(
                (K_H1HL, h1_pair_lo),
                (K_LN, rstd1),
                (K_OHL, o_pair_lo),
                (K_EXP, e_pair_lo),
                (K_H0, h0_pair_lo),
                (K_XHI_A, x_pair_lo(0)),
                (K_XHI_B, x_pair_lo(1)),
            )

            def slot(j, q):
                for k, stage in stages:
                    at = group_of(j, q, k)
                    if at is not None:
                        stage(j, *at)

            run_slots(pool, slot)

            for n in range(PAIRS):
                w = slice(2 * n, 2 * n + 2)
                pool.wait_ge(mv2_ready, 2 * n + 2)
                nc.gpsimd.tensor_scalar(veps2[:, w], mv2[:, w, 1], EPS, None, ALU.add).then_inc(ve2_ready, 1)
                pool.wait_ge(ve2_ready, n + 1)
                nc.gpsimd.tensor_tensor(rstd2[:, w], veps2[:, w], minus_half[:].broadcast_to([P, 2]), ALU.pow).then_inc(rstd2_ready, 1)


def kernel(x, L0_tok_W, L0_tok_b, L0_attn_Wqkv, L0_attn_Wout, L0_attn_Wpos, L0_attn_coeffs,
           L0_ffn_wf, L0_ffn_uf, L0_ffn_bf, L0_ffn_wi, L0_ffn_ui, L0_ffn_bi, L0_ffn_wc, L0_ffn_uc, L0_ffn_bc,
           L0_ffn_wo, L0_ffn_uo, L0_ffn_bo, L0_ffn_in_c):
    import numpy as np
    import concourse.bacc as bacc
    from concourse.bass_utils import run_bass_kernel_spmd

    def rows(w, chunks):
        w = np.asarray(w)
        return np.ascontiguousarray(w.T.reshape(chunks, P, w.shape[0]).transpose(1, 0, 2).reshape(P, -1))

    def gates_of(ws):
        w = np.stack([np.asarray(a) for a in ws])
        w = w.reshape(NG, KC, P, KC, P).transpose(4, 3, 1, 0, 2)
        return np.ascontiguousarray(w.reshape(P, -1))

    x = np.asarray(x)
    blocks = x.reshape(x.shape[0], 3, 4, 16, 4, 16).transpose(0, 1, 2, 4, 3, 5)
    patches = blocks.reshape(G, TOK, PC, P)
    xT = np.ascontiguousarray(patches.transpose(3, 0, 2, 1).reshape(P, -1))
    gb = np.stack([np.asarray(a) for a in (L0_ffn_bf, L0_ffn_bi, L0_ffn_bc)]).reshape(NG, KC, P).transpose(1, 0, 2)
    brow = np.concatenate([np.asarray(L0_tok_b), gb.reshape(-1), np.asarray(L0_ffn_bo)]).reshape(1, -1).repeat(2, 0)

    idx = np.clip(np.round(np.arange(S, dtype=np.float32) / np.float32(S - 1) * (RES - 1)).astype(int), 0, RES - 1)
    ramp = np.linspace(0.0, 1.0, RES).astype(np.float32)
    lag = idx[None, :] - np.arange(TAPS)[:, None]
    protoT = np.where(lag >= 0, ramp[np.maximum(lag, 0)], 0).astype(np.float32)
    i, jj, d = np.meshgrid(np.arange(S), np.arange(S), np.arange(S), indexing="ij")
    pick = np.tile((np.abs(i - jj) == d).astype(np.float32).reshape(S, S * S), (HC, 1))

    blocks16 = np.repeat(np.eye(HC, dtype=np.float32), HD, axis=0)

    arrays = {
        "xT": xT, "w_tok": rows(L0_tok_W, PC), "w_qkv": rows(L0_attn_Wqkv, KC), "w_out": rows(L0_attn_Wout, KC),
        "w_gx": gates_of((L0_ffn_wf, L0_ffn_wi, L0_ffn_wc)), "w_gu": gates_of((L0_ffn_uf, L0_ffn_ui, L0_ffn_uc)),
        "w_ox": rows(L0_ffn_wo, KC), "w_ou": rows(L0_ffn_uo, KC), "brow": brow,
        "in_c": np.ascontiguousarray(np.asarray(L0_ffn_in_c).reshape(KC, P).T),
        "coeffs": np.asarray(L0_attn_coeffs), "wpos": np.ascontiguousarray(np.asarray(L0_attn_Wpos).T),
        "protoT": protoT, "pick": pick, "blocks": blocks16, "eye": np.eye(P, dtype=np.float32),
    }
    nc = bacc.Bacc("TRN2", target_bir_lowering=False, num_devices=1)
    args = {n: nc.dram_tensor(n + "_dram", a.shape, mybir.dt.from_np(a.dtype), kind="ExternalInput").ap()
            for n, a in arrays.items()}
    out = nc.dram_tensor("out_dram", (G * TOK, D), F32, kind="ExternalOutput").ap()
    vit_layer(nc, **args, out=out)
    r = run_bass_kernel_spmd(nc, [{n + "_dram": a for n, a in arrays.items()}], core_ids=[0])
    return r.results[0]["out_dram"].reshape(x.shape[0], S, D)
```
